# Optimizing a Trainium2 kernel written in Bass

```python
import numpy as np
import jax
import jax.numpy as jnp

def _softmax(x, axis=-1):
    return jax.nn.softmax(x, axis=axis)

def _gelu(x):
    return jax.nn.gelu(x, approximate=True)

def _silu(x):
    return jax.nn.silu(x)

def _sigmoid(x):
    return jax.nn.sigmoid(x)

def _layernorm(x, axis=-1, eps=1e-05):
    m = jnp.mean(x, axis=axis, keepdims=True)
    v = jnp.var(x, axis=axis, keepdims=True)
    return (x - m) / jnp.sqrt(v + eps)

def _scatter_add(tgt, idx, src, axis=0):
    return tgt.at[idx].add(src)

def _segment_sum(src, seg, n):
    return jax.ops.segment_sum(src, seg, n)
kernel_name = 'mk_dlrm_tower_d1_rec_r8_0c9b43'

def setup_inputs(seed: int=0):
    np.random.seed(seed)
    _w = jnp.asarray

    def _rec_inputs():
        import jax
        import jax.numpy as jnp
        _tk = jax.random.key(seed)
        dense_ctx = jax.random.normal(jax.random.fold_in(_tk, 190), (512, 16), jnp.float32)
        ids = jnp.stack([jax.random.randint(jax.random.fold_in(_tk, 200 + f), (512,), 0, v, jnp.int32) for f, v in enumerate([12500, 12500, 1250, 12500, 1250, 1250, 12500, 1250, 125000, 1250, 1000, 1000, 12500, 1250, 125000, 1250, 125000, 1000, 12500, 12500, 1250, 1250, 1000, 1250, 1000, 1250, 1250, 1250, 1000, 1000, 1250, 1000])], axis=1)
        tbl_0 = 0.05 * jax.random.normal(jax.random.fold_in(_tk, 500 + 0), (12500, 64), jnp.float32)
        tbl_1 = 0.05 * jax.random.normal(jax.random.fold_in(_tk, 500 + 1), (12500, 64), jnp.float32)
        tbl_2 = 0.05 * jax.random.normal(jax.random.fold_in(_tk, 500 + 2), (1250, 64), jnp.float32)
        tbl_3 = 0.05 * jax.random.normal(jax.random.fold_in(_tk, 500 + 3), (12500, 64), jnp.float32)
        tbl_4 = 0.05 * jax.random.normal(jax.random.fold_in(_tk, 500 + 4), (1250, 64), jnp.float32)
        tbl_5 = 0.05 * jax.random.normal(jax.random.fold_in(_tk, 500 + 5), (1250, 64), jnp.float32)
        tbl_6 = 0.05 * jax.random.normal(jax.random.fold_in(_tk, 500 + 6), (12500, 64), jnp.float32)
        tbl_7 = 0.05 * jax.random.normal(jax.random.fold_in(_tk, 500 + 7), (1250, 64), jnp.float32)
        tbl_8 = 0.05 * jax.random.normal(jax.random.fold_in(_tk, 500 + 8), (125000, 64), jnp.float32)
        tbl_9 = 0.05 * jax.random.normal(jax.random.fold_in(_tk, 500 + 9), (1250, 64), jnp.float32)
        tbl_10 = 0.05 * jax.random.normal(jax.random.fold_in(_tk, 500 + 10), (1000, 64), jnp.float32)
        tbl_11 = 0.05 * jax.random.normal(jax.random.fold_in(_tk, 500 + 11), (1000, 64), jnp.float32)
        tbl_12 = 0.05 * jax.random.normal(jax.random.fold_in(_tk, 500 + 12), (12500, 64), jnp.float32)
        tbl_13 = 0.05 * jax.random.normal(jax.random.fold_in(_tk, 500 + 13), (1250, 64), jnp.float32)
        tbl_14 = 0.05 * jax.random.normal(jax.random.fold_in(_tk, 500 + 14), (125000, 64), jnp.float32)
        tbl_15 = 0.05 * jax.random.normal(jax.random.fold_in(_tk, 500 + 15), (1250, 64), jnp.float32)
        tbl_16 = 0.05 * jax.random.normal(jax.random.fold_in(_tk, 500 + 16), (125000, 64), jnp.float32)
        tbl_17 = 0.05 * jax.random.normal(jax.random.fold_in(_tk, 500 + 17), (1000, 64), jnp.float32)
        tbl_18 = 0.05 * jax.random.normal(jax.random.fold_in(_tk, 500 + 18), (12500, 64), jnp.float32)
        tbl_19 = 0.05 * jax.random.normal(jax.random.fold_in(_tk, 500 + 19), (12500, 64), jnp.float32)
        tbl_20 = 0.05 * jax.random.normal(jax.random.fold_in(_tk, 500 + 20), (1250, 64), jnp.float32)
        tbl_21 = 0.05 * jax.random.normal(jax.random.fold_in(_tk, 500 + 21), (1250, 64), jnp.float32)
        tbl_22 = 0.05 * jax.random.normal(jax.random.fold_in(_tk, 500 + 22), (1000, 64), jnp.float32)
        tbl_23 = 0.05 * jax.random.normal(jax.random.fold_in(_tk, 500 + 23), (1250, 64), jnp.float32)
        tbl_24 = 0.05 * jax.random.normal(jax.random.fold_in(_tk, 500 + 24), (1000, 64), jnp.float32)
        tbl_25 = 0.05 * jax.random.normal(jax.random.fold_in(_tk, 500 + 25), (1250, 64), jnp.float32)
        tbl_26 = 0.05 * jax.random.normal(jax.random.fold_in(_tk, 500 + 26), (1250, 64), jnp.float32)
        tbl_27 = 0.05 * jax.random.normal(jax.random.fold_in(_tk, 500 + 27), (1250, 64), jnp.float32)
        tbl_28 = 0.05 * jax.random.normal(jax.random.fold_in(_tk, 500 + 28), (1000, 64), jnp.float32)
        tbl_29 = 0.05 * jax.random.normal(jax.random.fold_in(_tk, 500 + 29), (1000, 64), jnp.float32)
        tbl_30 = 0.05 * jax.random.normal(jax.random.fold_in(_tk, 500 + 30), (1250, 64), jnp.float32)
        tbl_31 = 0.05 * jax.random.normal(jax.random.fold_in(_tk, 500 + 31), (1000, 64), jnp.float32)
        _rk = jax.random.fold_in(_tk, 7)
        W_top1 = 0.0693375 * jax.random.normal(jax.random.fold_in(_tk, 801), (208, 512), jnp.float32)
        W_top2 = 0.0441942 * jax.random.normal(jax.random.fold_in(_tk, 802), (512, 256), jnp.float32)
        W_top3 = 0.0625 * jax.random.normal(jax.random.fold_in(_tk, 803), (256, 1), jnp.float32)
        b_top1 = jnp.zeros((512,), jnp.float32)
        b_top2 = jnp.zeros((256,), jnp.float32)
        return (dense_ctx, ids, tbl_0, tbl_1, tbl_2, tbl_3, tbl_4, tbl_5, tbl_6, tbl_7, tbl_8, tbl_9, tbl_10, tbl_11, tbl_12, tbl_13, tbl_14, tbl_15, tbl_16, tbl_17, tbl_18, tbl_19, tbl_20, tbl_21, tbl_22, tbl_23, tbl_24, tbl_25, tbl_26, tbl_27, tbl_28, tbl_29, tbl_30, tbl_31, W_top1, b_top1, W_top2, b_top2, W_top3)
    dense_ctx, ids, tbl_0, tbl_1, tbl_2, tbl_3, tbl_4, tbl_5, tbl_6, tbl_7, tbl_8, tbl_9, tbl_10, tbl_11, tbl_12, tbl_13, tbl_14, tbl_15, tbl_16, tbl_17, tbl_18, tbl_19, tbl_20, tbl_21, tbl_22, tbl_23, tbl_24, tbl_25, tbl_26, tbl_27, tbl_28, tbl_29, tbl_30, tbl_31, W_top1, b_top1, W_top2, b_top2, W_top3 = _rec_inputs()

    def _L0_rec_setup():
        import jax, jax.numpy as jnp
        import numpy as np
        B, F, D = (256, 32, 64)
        LAYER_SIZE = (128, 128)

        def _cin_layer(h, x0, W, b):
            bsz, H, d = h.shape
            M = x0.shape[1]
            z = jnp.einsum('bhd,bmd->bhmd', h, x0).reshape(bsz, H * M, d)
            out = jnp.einsum('bcd,oc->bod', z, W) + b[None, :, None]
            return jax.nn.relu(out)
        key = jax.random.key(seed)
        k1, k2, k3 = jax.random.split(key, 3)
        inputs = jax.random.normal(k1, (B, F, D), dtype=jnp.float32)
        W0 = jax.random.normal(k2, (LAYER_SIZE[0], F * F), dtype=jnp.float32) * 0.03
        b0 = jnp.zeros((LAYER_SIZE[0],), dtype=jnp.float32)
        W1 = jax.random.normal(k3, (LAYER_SIZE[1], LAYER_SIZE[0] // 2 * F), dtype=jnp.float32) * 0.03
        b1 = jnp.zeros((LAYER_SIZE[1],), dtype=jnp.float32)
        return {'inputs': inputs, 'W0': W0, 'b0': b0, 'W1': W1, 'b1': b1}
    _L0_rec_all = _L0_rec_setup()
    _L0_rec_in = {k: v for k, v in _L0_rec_all.items() if k in ('W0', 'b0', 'W1', 'b1')}
    del _L0_rec_all
    return {'dense_ctx': dense_ctx, 'ids': ids, 'tbl_0': tbl_0, 'tbl_1': tbl_1, 'tbl_2': tbl_2, 'tbl_3': tbl_3, 'tbl_4': tbl_4, 'tbl_5': tbl_5, 'tbl_6': tbl_6, 'tbl_7': tbl_7, 'tbl_8': tbl_8, 'tbl_9': tbl_9, 'tbl_10': tbl_10, 'tbl_11': tbl_11, 'tbl_12': tbl_12, 'tbl_13': tbl_13, 'tbl_14': tbl_14, 'tbl_15': tbl_15, 'tbl_16': tbl_16, 'tbl_17': tbl_17, 'tbl_18': tbl_18, 'tbl_19': tbl_19, 'tbl_20': tbl_20, 'tbl_21': tbl_21, 'tbl_22': tbl_22, 'tbl_23': tbl_23, 'tbl_24': tbl_24, 'tbl_25': tbl_25, 'tbl_26': tbl_26, 'tbl_27': tbl_27, 'tbl_28': tbl_28, 'tbl_29': tbl_29, 'tbl_30': tbl_30, 'tbl_31': tbl_31, 'W_top1': W_top1, 'b_top1': b_top1, 'W_top2': W_top2, 'b_top2': b_top2, 'W_top3': W_top3, 'L0_rec_W0': _L0_rec_in['W0'], 'L0_rec_b0': _L0_rec_in['b0'], 'L0_rec_W1': _L0_rec_in['W1'], 'L0_rec_b1': _L0_rec_in['b1']}

def reference(dense_ctx, ids, tbl_0, tbl_1, tbl_2, tbl_3, tbl_4, tbl_5, tbl_6, tbl_7, tbl_8, tbl_9, tbl_10, tbl_11, tbl_12, tbl_13, tbl_14, tbl_15, tbl_16, tbl_17, tbl_18, tbl_19, tbl_20, tbl_21, tbl_22, tbl_23, tbl_24, tbl_25, tbl_26, tbl_27, tbl_28, tbl_29, tbl_30, tbl_31, W_top1, b_top1, W_top2, b_top2, W_top3, L0_rec_W0, L0_rec_b0, L0_rec_W1, L0_rec_b1):
    import jax
    import jax.numpy as jnp

    def _L0_rec_ref(inputs, W0, b0, W1, b1):
        import jax, jax.numpy as jnp
        import numpy as np
        B, F, D = (256, 32, 64)
        LAYER_SIZE = (128, 128)

        def _cin_layer(h, x0, W, b):
            bsz, H, d = h.shape
            M = x0.shape[1]
            z = jnp.einsum('bhd,bmd->bhmd', h, x0).reshape(bsz, H * M, d)
            out = jnp.einsum('bcd,oc->bod', z, W) + b[None, :, None]
            return jax.nn.relu(out)
        out0 = _cin_layer(inputs, inputs, W0, b0)
        half = LAYER_SIZE[0] // 2
        next_hidden = out0[:, :half, :]
        direct0 = out0[:, half:, :]
        direct1 = _cin_layer(next_hidden, inputs, W1, b1)
        result = jnp.concatenate([direct0, direct1], axis=1)
        return jnp.sum(result, axis=-1)
    e = jnp.stack([tbl_0[ids[:, 0]], tbl_1[ids[:, 1]], tbl_2[ids[:, 2]], tbl_3[ids[:, 3]], tbl_4[ids[:, 4]], tbl_5[ids[:, 5]], tbl_6[ids[:, 6]], tbl_7[ids[:, 7]], tbl_8[ids[:, 8]], tbl_9[ids[:, 9]], tbl_10[ids[:, 10]], tbl_11[ids[:, 11]], tbl_12[ids[:, 12]], tbl_13[ids[:, 13]], tbl_14[ids[:, 14]], tbl_15[ids[:, 15]], tbl_16[ids[:, 16]], tbl_17[ids[:, 17]], tbl_18[ids[:, 18]], tbl_19[ids[:, 19]], tbl_20[ids[:, 20]], tbl_21[ids[:, 21]], tbl_22[ids[:, 22]], tbl_23[ids[:, 23]], tbl_24[ids[:, 24]], tbl_25[ids[:, 25]], tbl_26[ids[:, 26]], tbl_27[ids[:, 27]], tbl_28[ids[:, 28]], tbl_29[ids[:, 29]], tbl_30[ids[:, 30]], tbl_31[ids[:, 31]]], axis=1)
    z = _L0_rec_ref(e, L0_rec_W0, L0_rec_b0, L0_rec_W1, L0_rec_b1)
    z = z.reshape(z.shape[0], -1)
    h = jnp.concatenate([z, dense_ctx], axis=1)
    h = jnp.maximum(h @ W_top1 + b_top1, 0.0)
    h = jnp.maximum(h @ W_top2 + b_top2, 0.0)
    y = h @ W_top3
    return y

_drawn_inputs = setup_inputs


def setup_inputs(seed=0):
    import zlib

    import numpy as np

    out = dict(_drawn_inputs(seed))
    spreads = {'b_top1': (0.0, 2.0),
     'b_top2': (0.0, 2.0),
     'L0_rec_b0': (0.0, 0.1),
     'L0_rec_b1': (0.0, 0.571)}
    factors = {'tbl_0': 8.0,
     'tbl_1': 8.0,
     'tbl_2': 8.0,
     'tbl_3': 8.0,
     'tbl_4': 8.0,
     'tbl_5': 8.0,
     'tbl_6': 8.0,
     'tbl_7': 8.0,
     'tbl_8': 8.0,
     'tbl_9': 8.0,
     'tbl_10': 8.0,
     'tbl_11': 8.0,
     'tbl_12': 8.0,
     'tbl_13': 8.0,
     'tbl_14': 8.0,
     'tbl_15': 8.0,
     'tbl_16': 8.0,
     'tbl_17': 8.0,
     'tbl_18': 8.0,
     'tbl_19': 8.0,
     'tbl_20': 8.0,
     'tbl_21': 8.0,
     'tbl_22': 8.0,
     'tbl_23': 8.0,
     'tbl_24': 8.0,
     'tbl_25': 8.0,
     'tbl_26': 8.0,
     'tbl_27': 8.0,
     'tbl_28': 8.0,
     'tbl_29': 8.0,
     'tbl_30': 8.0,
     'tbl_31': 8.0,
     'L0_rec_W0': 8.0,
     'L0_rec_W1': 7.781,
     'dense_ctx': 8.0}
    for name, (base, spread) in spreads.items():
        noise = np.random.default_rng([zlib.crc32(name.encode()), seed]).standard_normal(out[name].shape)
        drawn = base * np.exp(spread * noise) if base else spread * noise
        out[name] = jnp.asarray(drawn.astype(out[name].dtype))
    for name, factor in factors.items():
        out[name] = (out[name] * factor).astype(out[name].dtype)
    return out
```

```python
from contextlib import ExitStack

import numpy as np

import concourse.bass as bass
from concourse import mybir

ALU = mybir.AluOpType
ACT = mybir.ActivationFunctionType
AX_X = mybir.AxisListType.X
F32 = mybir.dt.float32
F32R = mybir.dt.float32r
U32 = mybir.dt.uint32

P = 128
F = 32
D = 64
O = 128
H = O // 2
TB = 8
N = TB * D
Q = 4
FQ = F // Q
C0 = 5
C1 = H * F // P
NBUF = 4
ZBUF = 4
LAG = 3
GMAX = 3

ORDER1 = [(n % Q) * (C1 // Q) + n // Q for n in range(C1)]
SLOTS = [(0, [0, 1, 2]), (0, [3, 4])]
for a, b in ((0, 3), (3, 6), (6, 9), (9, 12), (12, 14), (14, 16)):
    SLOTS.append((1, ORDER1[a:b]))
S = len(SLOTS)
POOL_SHARE = [2, 1, 2, 2, 2, 2, 1, 1]


def slots_of(i, tiles):
    return [s for s in range(S) if (s >= 2 or i < tiles) and (s < 2 or i > 0)]


def constants():
    row_f = np.full(P, -1)
    for q in range(Q):
        for part in range(2):
            for m in range(FQ):
                row_f[q * 32 + part * FQ + m] = q * FQ + m
    sel0 = np.zeros((P, C0, P), np.float32)
    for k in range(C0):
        for g in range(4):
            for i in range(F):
                shift = 16 if k == 4 else 4 * k + g
                sel0[row_f == (i + shift) % F, k, g * F + i] = 1.0
    sel1 = np.zeros((P, C1 // Q, P), np.float32)
    for c in range(C1 // Q):
        for j in range(2):
            sel1[(row_f >= 0) & (row_f % FQ == 2 * c + j), c, j * H:(j + 1) * H] = 1.0
    both = np.concatenate([sel0, sel1, np.eye(P, dtype=np.float32)[:, None, :]], axis=1)
    return np.ascontiguousarray(both.reshape(P, -1))


def dlrm_tower(nc, dense, ids, tables, Wt1, bt1, Wt2, bt2, Wt3, W0, b0, W1, b1, consts, out):
    B, ND = dense.shape
    TILES = B // TB
    BG = B // P
    M1, M2 = Wt1.shape[1], Wt2.shape[1]
    K1, K2 = M1 // P, M2 // P
    NC = C0 + C1 // Q + 1

    x_dram = nc.dram_tensor("x_dram", (F, B, D), F32).ap()
    parts_dram = nc.dram_tensor("parts_dram", (Q, 2, FQ, B, D), F32).ap()

    def group(i, s):
        if isinstance(i, int) and i == 0:
            return s
        if isinstance(i, int) and i == TILES:
            return S * i - S + s
        return S * i + (s + 2 - S)

    def residue(model, s, n):
        edge = model in (0, TILES)
        return (s if edge else s + 2) % n

    everything = [(i, s) for i in range(TILES + 1) for s in slots_of(i, TILES)]

    def before(i, model, s, lag):
        at = everything.index((model, s)) - lag
        if at < 0:
            return None
        mi, ms = everything[at]
        return i + (mi - model) if mi != model else i, mi, ms

    with ExitStack() as ctx:
        def sb(name, shape, dt=F32):
            return ctx.enter_context(nc.sbuf_tensor(name, shape, dt))

        def pb(name, shape):
            return ctx.enter_context(nc.psum_tensor(name, shape, F32))

        def sem(name):
            return ctx.enter_context(nc.semaphore(name))

        idx = sb("idx", [P, BG, F], mybir.dt.int32)
        emb = sb("emb", [P, BG, F, D])
        emb_hi = sb("emb_hi", [P, F, D], F32R)
        emb_lo = sb("emb_lo", [P, F, D], F32R)
        const = sb("const", [P, NC, P])
        sel = sb("sel", [P, NC - 1, P], F32R)
        ident = const[:, NC - 1, :]
        w0s = sb("w0s", [P, 20, F])
        w_hi = sb("w_hi", [P, C0 + C1, P], F32R)
        w_lo = sb("w_lo", [P, C0 + C1, P], F32R)
        b0_sb = sb("b0_sb", [P, 1])
        b1_sb = sb("b1_sb", [P, 1])
        x4 = sb("x4", [P, NBUF, N])
        parts = sb("parts", [P, NBUF, N], F32R)
        hid = sb("hid", [P, NBUF, N])
        z = sb("z", [P, ZBUF, GMAX, N])
        z_flat = z[:, :, :, :].rearrange("p b k n -> p (b k n)")
        w0 = z_flat[:, 0:F * F]
        w1 = z_flat[:, F * F:F * F + H * F].rearrange("p (h m) -> p h m", m=F)
        w1s = z_flat[:, F * F + H * F:F * F + 2 * H * F].rearrange("p (m h) -> p m h", h=H)
        z_hi = sb("z_hi", [P, ZBUF, GMAX, N], F32R)
        z_lo = sb("z_lo", [P, ZBUF, GMAX, N], F32R)
        direct0 = sb("direct0", [P, N])
        direct1 = sb("direct1", [P, N])
        dense_sb = sb("dense_sb", [P, BG, ND])
        zA = sb("zA", [P, B])
        zB = sb("zB", [P, B])
        wtA = sb("wtA", [P, M1])
        wtB = sb("wtB", [P, M1])
        wt2 = sb("wt2", [P, K1, M2])
        wt3 = sb("wt3", [P, K2])
        bt1_sb = sb("bt1_sb", [P, K1])
        bt2_sb = sb("bt2_sb", [P, K2])
        h1 = emb[:, 0, :, :].rearrange("p f d -> p (f d)").rearrange("p (k b) -> p k b", k=K1)
        h2 = emb[:, 1, 0:K2 * B // D, :].rearrange("p f d -> p (f d)").rearrange("p (k b) -> p k b", k=K2)
        y = sb("y", [1, B])

        spread = [pb("spread0", [P, GMAX, N]), pb("spread1", [P, GMAX, N])]
        out0 = pb("out0", [P, N])
        out1 = pb("out1", [P, N])
        mlp3 = spread[1][0:1, 1, :]

        def mlp1(k):
            return spread[k // GMAX][:, k % GMAX, :]

        def mlp2(k):
            return (out0, out1)[k][:, :]

        idx_in = sem("idx_in")
        gathered = [sem(f"gathered{g}") for g in range(BG)]
        cut_hi = sem("cut_hi")
        cut_lo = sem("cut_lo")
        stored_x = sem("stored_x")
        stored_hi = sem("stored_hi")
        stored_lo = sem("stored_lo")
        w_in = sem("w_in")
        c_in = sem("c_in")
        m_in = sem("m_in")
        dense_t_done = sem("dense_t_done")
        hid_done = sem("hid_done")
        zeroed = sem("zeroed")
        parts_zeroed = sem("parts_zeroed")
        sel_done = sem("sel_done")
        w0s_done = sem("w0s_done")
        w1s_done = sem("w1s_done")
        transposed = sem("transposed")
        w_hi_done = sem("w_hi_done")
        w_lo_done = sem("w_lo_done")
        rem_w_done = sem("rem_w_done")
        dense_done = sem("dense_done")
        x_in = [sem(f"x_in{k}") for k in range(NBUF)]
        spread_done = sem("spread_done")
        mult_done = sem("mult_done")
        hi_done = sem("hi_done")
        pool_lo_done = sem("pool_lo_done")
        dve_lo_done = sem("dve_lo_done")
        prod_done = sem("prod_done")
        out0_read = sem("out0_read")
        out1_read = sem("out1_read")
        sum0_done = sem("sum0_done")
        sum1_done = sem("sum1_done")
        m1_done = sem("m1_done")
        h1_done = sem("h1_done")
        m2_done = sem("m2_done")
        h2_done = sem("h2_done")
        m3_done = sem("m3_done")
        y_done = sem("y_done")
        y_out = sem("y_out")

        LOADS = 16 * (Q + Q)
        FIRST, LAST = 2, TILES - 2
        assert (LAST - FIRST) % NBUF == 0

        def iterations(eng, body):
            for i in range(FIRST):
                body(i, i)
            with eng.Fori(0, (LAST - FIRST) // NBUF) as turn:
                for r in range(NBUF):
                    body(turn * NBUF + (FIRST + r), FIRST + NBUF + r)
            for i in range(LAST, TILES + 1):
                body(i, i)

        def landed(i, model):
            first = model % NBUF
            return (i - (first - NBUF)) * (LOADS // NBUF)

        block = ctx.enter_context(nc.Block())

        @block.sync
        def _(sp):
            sp.dma_start(idx[:, :, :], ids.rearrange("(g p) f -> p g f", p=P)).then_inc(idx_in, 16)
            sp.dma_start(const[:, :, :], consts.rearrange("p (n m) -> p n m", m=P)).then_inc(c_in, 16)
            sp.dma_start(w0, W0).then_inc(w_in, 16)
            sp.dma_start(w1, W1.rearrange("o (h m) -> o h m", m=F)).then_inc(w_in, 16)
            sp.dma_start(b0_sb[:, :], b0.rearrange("(o a) -> o a", a=1)).then_inc(m_in, 16)
            sp.dma_start(b1_sb[:, :], b1.rearrange("(o a) -> o a", a=1)).then_inc(m_in, 16)
            sp.dma_start(dense_sb[:, :, :], dense.rearrange("(g p) n -> p g n", p=P)).then_inc(m_in, 16)
            sp.wait_ge(zeroed, 2)
            sp.dma_start(wtA[0:ND, :], Wt1[3 * H:3 * H + ND, :]).then_inc(m_in, 16)
            sp.dma_start(wtA[H:P, :], Wt1[0:H, :]).then_inc(m_in, 16)
            sp.dma_start(wtB[:, :], Wt1[H:3 * H, :]).then_inc(m_in, 16)
            sp.dma_start(wt2[:, :, :], Wt2.rearrange("(k p) n -> p k n", p=P)).then_inc(m_in, 16)
            sp.dma_start(wt3[:, :], Wt3.rearrange("(k p) n -> p (k n)", p=P), allow_slow_non_contiguous=True).then_inc(m_in, 16)
            sp.dma_start(bt1_sb[:, :], bt1.rearrange("(k p) -> p k", p=P), allow_slow_non_contiguous=True).then_inc(m_in, 16)
            sp.dma_start(bt2_sb[:, :], bt2.rearrange("(k p) -> p k", p=P), allow_slow_non_contiguous=True).then_inc(m_in, 16)
            for g in range(BG):
                rows = slice(g * P, (g + 1) * P)
                sp.wait_ge(gathered[g], 16 * F)
                sp.dma_start(x_dram[:, rows, :].rearrange("f b d -> b f d"), emb[:, g, :, :]).then_inc(stored_x, 16)
                for part, (src, cut, stored) in enumerate(((emb_hi, cut_hi, stored_hi), (emb_lo, cut_lo, stored_lo))):
                    sp.wait_ge(cut, g + 1)
                    for q in range(Q):
                        sp.dma_start(parts_dram[q, part, :, rows, :].rearrange("m b d -> b m d"),
                                     src[:, q * FQ:(q + 1) * FQ, :].bitcast(F32)).then_inc(stored, 16)
            sp.wait_ge(parts_zeroed, 1)
            sp.wait_ge(stored_x, 16 * BG)
            sp.wait_ge(stored_hi, 16 * Q * BG)
            sp.wait_ge(stored_lo, 16 * Q * BG)

            x_cols = x_dram.rearrange("f b d -> f (b d)")
            p_cols = parts_dram.rearrange("q r m b d -> q (r m) (b d)")

            def load(i, model):
                buf = model % NBUF
                cols = bass.ds(i * N, N)
                for q in range(Q):
                    sp.dma_start(x4[q * 32:q * 32 + F, buf, :], x_cols[:, cols]).then_inc(x_in[buf], 16)
                    sp.dma_start(parts[q * 32:q * 32 + 2 * FQ, buf, :].bitcast(F32), p_cols[q, :, cols]).then_inc(x_in[buf], 16)

            for i in range(NBUF):
                load(i, i)

            def body(i, model):
                if 0 < model <= TILES - NBUF:
                    sp.wait_ge(spread_done, group(i, S - 1) + 1)
                    load(i + (NBUF - 1), model + NBUF - 1)

            body(1, 1)
            with sp.Fori(0, (LAST - FIRST) // NBUF - 1) as turn:
                for r in range(NBUF):
                    body(turn * NBUF + (FIRST + r), FIRST + NBUF + r)
            for i in range(LAST - NBUF, TILES):
                body(i, i)

            sp.wait_ge(y_done, 1)
            sp.dma_start(out.rearrange("(a b) n -> a (b n)", a=1), y[:, :]).then_inc(y_out, 16)
            sp.wait_ge(y_out, 16)

        @block.gpsimd
        def _(pool):
            nc.gpsimd.memset(wtA[:, :], 0.0).then_inc(zeroed, 1)
            nc.gpsimd.memset(zA[:, :], 0.0).then_inc(zeroed, 1)
            pool.wait_ge(idx_in, 16)
            for g in range(BG):
                for f in range(F):
                    pool.indirect_dma_start(
                        emb[:, g, f, :], None, tables[f],
                        bass.IndirectOffsetOnAxis(ap=idx[:, g, f:f + 1].bitcast(U32), axis=0),
                    ).then_inc(gathered[g], 16)

            def body(i, model):
                for s in slots_of(model, TILES):
                    n, buf = group(i, s), residue(model, s, ZBUF)
                    k = POOL_SHARE[s]
                    pool.wait_ge(hi_done, n + 1)
                    nc.gpsimd.tensor_tensor(z_lo[:, buf, 0:k, :], z[:, buf, 0:k, :],
                                            z_hi[:, buf, 0:k, :].bitcast(F32), ALU.subtract).then_inc(pool_lo_done, 1)

            iterations(pool, body)

        @block.scalar
        def _(act):
            act.wait_ge(w_in, 32)
            nc.scalar.activation(w1s.rearrange("p m h -> p h m"), w1, ACT.Copy).then_inc(w1s_done, 1)
            act.wait_ge(c_in, 16)
            nc.scalar.activation(sel[:, :, :], const[:, 0:NC - 1, :], ACT.Copy).then_inc(sel_done, 1)
            for c in range(0, C0 + C1, GMAX):
                act.wait_ge(transposed, c // GMAX + 1)
                nc.scalar.activation(w_hi[:, c:c + GMAX, :], spread[c // GMAX % 2][:, :, 0:P], ACT.Copy).then_inc(w_hi_done, 1)
            for g in range(BG):
                act.wait_ge(gathered[g], 16 * F)
                if g:
                    act.wait_ge(stored_hi, 16 * Q * g)
                    act.wait_ge(cut_lo, g)
                nc.scalar.activation(emb_hi[:, :, :], emb[:, g, :, :], ACT.Copy).then_inc(cut_hi, 1)
            act.wait_ge(m_in, 16 * 10)

            def evacuate0(i, model):
                act.wait_ge(prod_done, group(i, 1) + 1)
                buf = model % NBUF
                nc.scalar.activation(hid[0:H, buf, :], out0[0:H, :], ACT.Relu, bias=b0_sb[0:H, :])
                nc.scalar.activation(hid[H:P, buf, :], out0[0:H, :], ACT.Relu, bias=b0_sb[0:H, :]).then_inc(hid_done, 1)
                if model:
                    act.wait_ge(sum0_done, i)
                nc.scalar.activation(direct0[H:P, :], out0[H:P, :], ACT.Relu, bias=b0_sb[H:P, :]).then_inc(out0_read, 1)

            def evacuate1(t, model):
                act.wait_ge(prod_done, group(t + 1, S - 1) + 1)
                if model:
                    act.wait_ge(sum1_done, t)
                nc.scalar.activation(direct1[:, :], out1[:, :], ACT.Relu, bias=b1_sb[:, :]).then_inc(out1_read, 1)

            def body(i, model):
                for s in slots_of(model, TILES):
                    n, buf, k = group(i, s), residue(model, s, ZBUF), len(SLOTS[s][1])
                    act.wait_ge(mult_done, n + 1)
                    if before(i, model, s, ZBUF):
                        act.wait_ge(prod_done, n + (1 - ZBUF))
                    nc.scalar.activation(z_hi[:, buf, 0:k, :], z[:, buf, 0:k, :], ACT.Copy).then_inc(hi_done, 1)
                    if s == (1 if model == 0 else 5) and model < TILES:
                        evacuate0(i, model)
                    if s == (5 if model == TILES else 3) and model >= 2:
                        evacuate1(i - 2, model - 2)

            iterations(act, body)
            evacuate1(TILES - 1, TILES - 1)

            for k in range(K1):
                act.wait_ge(m1_done, k + 1)
                nc.scalar.activation(h1[:, k, :], mlp1(k), ACT.Relu, bias=bt1_sb[:, k:k + 1]).then_inc(h1_done, 1)
            for k in range(K2):
                act.wait_ge(m2_done, k + 1)
                nc.scalar.activation(h2[:, k, :], mlp2(k), ACT.Relu, bias=bt2_sb[:, k:k + 1]).then_inc(h2_done, 1)
            act.wait_ge(m3_done, 1)
            nc.scalar.activation(y[:, :], mlp3, ACT.Copy).then_inc(y_done, 1)

        @block.vector
        def _(dve):
            nc.vector.memset(parts[:, :, :].bitcast(F32), 0.0).then_inc(parts_zeroed, 1)
            dve.wait_ge(w_in, 32)
            step = F + 1

            def run(at, n):
                return w0[:, at:at + step * (n - 1) + 1:step]

            nc.vector.tensor_copy(w0s[:, 0, :], run(0, F))
            for s in range(1, F // 2):
                nc.vector.tensor_tensor(w0s[:, s, 0:F - s], run(s, F - s), run(F * s, F - s), ALU.add)
                nc.vector.tensor_tensor(w0s[:, s, F - s:F], run(F * (F - s), s), run(F - s, s), ALU.add)
            for r in range(4):
                nc.vector.tensor_copy(w0s[:, 16 + r, 0:F // 2], run(F // 2, F // 2))
                last = nc.vector.tensor_copy(w0s[:, 16 + r, F // 2:F], run(F * (F // 2), F // 2))
            last.then_inc(w0s_done, 1)

            for c in range(0, C0 + C1, GMAX):
                dve.wait_ge(w_hi_done, c // GMAX + 1)
                nc.vector.tensor_tensor(w_lo[:, c:c + GMAX, :], spread[c // GMAX % 2][:, :, 0:P],
                                        w_hi[:, c:c + GMAX, :].bitcast(F32), ALU.subtract).then_inc(w_lo_done, 1)
            dve.wait_ge(w_lo_done, (C0 + C1) // GMAX)
            for a in (F, 3 * F):
                last = nc.vector.tensor_copy(w_hi[a:a + F, C0 - 1, :], w_lo[a:a + F, C0 - 1, :])
            last.then_inc(rem_w_done, 1)
            dve.wait_ge(zeroed, 2)
            dve.wait_ge(dense_t_done, 1)
            nc.vector.tensor_copy(zA[0:ND, :], out0[0:ND, :]).then_inc(dense_done, 1)

            for g in range(BG):
                dve.wait_ge(cut_hi, g + 1)
                if g:
                    dve.wait_ge(stored_lo, 16 * Q * g)
                nc.vector.tensor_tensor(emb_lo[:, :, :], emb[:, g, :, :], emb_hi[:, :, :].bitcast(F32),
                                        ALU.subtract).then_inc(cut_lo, 1)

            def low_parts(i, model, s):
                n, buf, k = group(i, s), residue(model, s, ZBUF), len(SLOTS[s][1])
                a = POOL_SHARE[s]
                dve.wait_ge(hi_done, n + 1)
                if s == 1:
                    nc.vector.tensor_tensor(z_hi[H:P, buf, 1, :], z[H:P, buf, 1, :], z_hi[H:P, buf, 1, :].bitcast(F32),
                                            ALU.subtract).then_inc(dve_lo_done, 1)
                else:
                    nc.vector.tensor_tensor(z_lo[:, buf, a:k, :], z[:, buf, a:k, :], z_hi[:, buf, a:k, :].bitcast(F32),
                                            ALU.subtract).then_inc(dve_lo_done, 1)

            def sum_over_d(dst, src, i, done):
                nc.vector.tensor_reduce(dst[:, bass.ds(i * TB, TB)], src.rearrange("p (b d) -> p b d", d=D),
                                        AX_X, ALU.add).then_inc(done, 1)

            def body(i, model):
                for s in slots_of(model, TILES):
                    n, buf, k = group(i, s), residue(model, s, ZBUF), len(SLOTS[s][1])
                    layer = SLOTS[s][0]
                    dve.wait_ge(spread_done, n + 1)
                    if layer == 0 and s == 0:
                        dve.wait_ge(x_in[model % NBUF], landed(i, model))
                    if s == 2:
                        dve.wait_ge(hid_done, i)
                    if before(i, model, s, ZBUF):
                        dve.wait_ge(pool_lo_done, n + (1 - ZBUF))
                    factor = x4[:, model % NBUF, :] if layer == 0 else hid[:, (model - 1) % NBUF, :]
                    nc.vector.tensor_tensor(z[:, buf, 0:k, :], spread[s % 2][:, 0:k, :],
                                            factor.unsqueeze(1).broadcast_to([P, k, N]), ALU.mult).then_inc(mult_done, 1)
                    if (one := before(i, model, s, 1)):
                        low_parts(*one)
                    if s == 7 and 0 < model < TILES:
                        dve.wait_ge(out0_read, i + 1)
                        sum_over_d(zA[H:P, :], direct0[H:P, :], i, sum0_done)
                    if s == 3 and model == 1:
                        dve.wait_ge(out0_read, 1)
                        sum_over_d(zA[H:P, :], direct0[H:P, :], 0, sum0_done)
                    if s == (7 if model == TILES else 5) and model >= 2:
                        dve.wait_ge(out1_read, i - 1)
                        sum_over_d(zB, direct1[:, :], i - 2, sum1_done)

            iterations(dve, body)
            low_parts(TILES, TILES, S - 1)
            dve.wait_ge(out1_read, TILES)
            sum_over_d(zB, direct1[:, :], TILES - 1, sum1_done)

        @block.tensor
        def _(pe):
            pe.wait_ge(c_in, 16)
            pe.wait_ge(w0s_done, 1)
            pe.wait_ge(w1s_done, 1)
            for c in range(C0 + C1):
                at = c // GMAX
                if c % GMAX == 0 and at >= 2:
                    pe.wait_ge(w_lo_done, at - 1)
                src = w0s[:, 4 * c:4 * c + 4, :] if c < C0 else w1s[:, 2 * (c - C0):2 * (c - C0) + 2, :]
                last = nc.tensor.transpose(spread[at % 2][:, c % GMAX, 0:P], src, ident)
                if c % GMAX == GMAX - 1:
                    last.then_inc(transposed, 1)
            pe.wait_ge(m_in, 16 * 10)
            for g in range(BG):
                last = nc.tensor.transpose(out0[0:ND, g * P:(g + 1) * P], dense_sb[:, g, :], ident)
            last.then_inc(dense_t_done, 1)
            pe.wait_ge(sel_done, 1)
            pe.wait_ge(rem_w_done, 1)
            pe.wait_ge(dense_done, 1)

            def spread_group(i, model, s):
                layer, chunks = SLOTS[s]
                if s == 0:
                    pe.wait_ge(x_in[model % NBUF], landed(i, model))
                if before(i, model, s, 2):
                    pe.wait_ge(mult_done, group(i, s) - 1)
                for at, c in enumerate(chunks):
                    if layer == 0:
                        w, x = sel[:, c, :], parts[:, model % NBUF, :]
                    else:
                        q, buf = c // (C1 // Q), (model - 1) % NBUF
                        w, x = sel[32 * q:32 * q + 32, C0 + c % (C1 // Q), :], parts[32 * q:32 * q + 32, buf, :]
                    last = nc.tensor.matmul(spread[s % 2][:, at, :], w, x, start=True, stop=True)
                last.then_inc(spread_done, 1)

            def products(i, model, s):
                layer, chunks = SLOTS[s]
                buf, base, out_bank = residue(model, s, ZBUF), (0, C0)[layer], (out0, out1)[layer]
                if s == 0 and model > 0:
                    pe.wait_ge(out0_read, i)
                if s == 2 and model > 1:
                    pe.wait_ge(out1_read, i - 1)
                pe.wait_ge(pool_lo_done, group(i, s) + 1)
                pe.wait_ge(dve_lo_done, group(i, s) + 1)
                passes = []
                for at, c in enumerate(chunks):
                    passes.append((w_hi[:, base + c, :], z_hi[:, buf, at, :]))
                    if not (layer == 0 and c == C0 - 1):
                        passes.append((w_lo[:, base + c, :], z_hi[:, buf, at, :]))
                        passes.append((w_hi[:, base + c, :], z_lo[:, buf, at, :]))
                for m, (w, x) in enumerate(passes):
                    last = nc.tensor.matmul(out_bank[:, :], w, x, start=(s in (0, 2) and m == 0),
                                            stop=(s in (1, 7) and m == len(passes) - 1))
                last.then_inc(prod_done, 1)

            def body(i, model):
                for s in slots_of(model, TILES):
                    spread_group(i, model, s)
                    if (old := before(i, model, s, LAG)):
                        products(*old)

            iterations(pe, body)
            for s in range(S - LAG, S):
                products(TILES, TILES, s)

            pe.wait_ge(sum0_done, TILES)
            pe.wait_ge(sum1_done, TILES)
            for k in range(K1):
                nc.tensor.matmul(mlp1(k), wtA[:, k * P:(k + 1) * P], zA[:, :], start=True, stop=False)
                nc.tensor.matmul(mlp1(k), wtB[:, k * P:(k + 1) * P], zB[:, :], start=False, stop=True).then_inc(m1_done, 1)
            for j in range(K2):
                for k in range(K1):
                    pe.wait_ge(h1_done, k + 1)
                    last = nc.tensor.matmul(mlp2(j), wt2[:, k, j * P:(j + 1) * P], h1[:, k, :], start=(k == 0), stop=(k == K1 - 1))
                last.then_inc(m2_done, 1)
            for k in range(K2):
                pe.wait_ge(h2_done, k + 1)
                last = nc.tensor.matmul(mlp3, wt3[:, k:k + 1], h2[:, k, :], start=(k == 0), stop=(k == K2 - 1))
            last.then_inc(m3_done, 1)


_INS = (["dense_ctx", "ids"] + [f"tbl_{f}" for f in range(F)]
        + ["W_top1", "b_top1", "W_top2", "b_top2", "W_top3", "L0_rec_W0", "L0_rec_b0", "L0_rec_W1", "L0_rec_b1"])


def kernel(**inputs):
    import numpy as _np
    import concourse.bacc as _bacc
    from concourse import mybir as _mybir
    from concourse.bass_utils import run_bass_kernel_spmd as _run

    nc = _bacc.Bacc("TRN2", target_bir_lowering=False, num_devices=1)
    arrays, aps = {}, []
    for name in _INS:
        a = _np.ascontiguousarray(inputs[name])
        arrays[f"in_{name}"] = a
        aps.append(nc.dram_tensor(f"in_{name}", a.shape, _mybir.dt.from_np(a.dtype), kind="ExternalInput").ap())
    c = constants()
    arrays["in_constants"] = c
    c_ap = nc.dram_tensor("in_constants", c.shape, _mybir.dt.from_np(c.dtype), kind="ExternalInput").ap()
    out = nc.dram_tensor("out", (inputs["ids"].shape[0], 1), _mybir.dt.float32, kind="ExternalOutput").ap()
    dlrm_tower(nc, aps[0], aps[1], aps[2:2 + F], *aps[2 + F:], c_ap, out)
    r = _run(nc, [arrays], core_ids=[0])
    return r.results[0]["out"]
```

```python
from contextlib import ExitStack

import numpy as np

import concourse.bass as bass
from concourse import mybir

ALU = mybir.AluOpType
ACT = mybir.ActivationFunctionType
AX_X = mybir.AxisListType.X
F32 = mybir.dt.float32
F32R = mybir.dt.float32r
U32 = mybir.dt.uint32

P = 128
F = 32
D = 64
O = 128
H = O // 2
TB = 8
N = TB * D
Q = 4
FQ = F // Q
C0 = 5
C1 = H * F // P
NBUF = 4
PAIR = 2
BANKS = 6
RING = 8
ZRING = 4
LAG = 5
READ0, SUM0, COPY0 = 6, 7, 7
READ1, SUM1 = 5, 6
GATHERS = ((3, 4), (1, 3), (1, 3), (0, 1))
AHEAD = 2

ORDER1 = [(n % Q) * (C1 // Q) + n // Q for n in range(C1)]
SLOTS = [
    (0, [0, 1], "vector", 2), (0, [2, 3], "pool", 4), (0, [4], "vector", 1), (1, ORDER1[0:2], "pool", 4),
    (1, ORDER1[2:4], "vector", 2), (1, ORDER1[4:6], "pool", 4), (1, ORDER1[6:8], "vector", 0),
    (1, ORDER1[8:10], "pool", 2), (1, ORDER1[10:12], "vector", 4), (1, ORDER1[12:14], "pool", 2),
    (1, ORDER1[14:16], "pool", 0),
]
S = len(SLOTS)
FIRST0, LAST0, FIRST1, LAST1 = 0, 2, 3, S - 1
POOL_SLOTS = [s for s in range(S) if SLOTS[s][2] == "pool"]


def rounds(total, most):
    short = -total % most
    full = (total - short * (most - 1)) // most
    assert full * most + short * (most - 1) == total and full >= 0
    return [b for r in range(full + short) for b in range(most if r < full else most - 1)]


PART_BUFFERS = rounds(NBUF * S, RING)
Z_BUFFERS = rounds(NBUF * len(POOL_SLOTS), ZRING)


def banks_of(s):
    return range(SLOTS[s][3], SLOTS[s][3] + len(SLOTS[s][1]))


def slots_of(i, tiles):
    return [s for s in range(S) if (i > 0 if SLOTS[s][0] else i < tiles)]


def constants():
    row_f = np.full(P, -1)
    for q in range(Q):
        for part in range(2):
            for m in range(FQ):
                row_f[q * 32 + part * FQ + m] = q * FQ + m
    sel0 = np.zeros((P, C0, P), np.float32)
    for k in range(C0):
        for g in range(4):
            for i in range(F):
                shift = 16 if k == 4 else 4 * k + g
                sel0[row_f == (i + shift) % F, k, g * F + i] = 1.0
    sel1 = np.zeros((P, C1 // Q, P), np.float32)
    for c in range(C1 // Q):
        for j in range(2):
            sel1[(row_f >= 0) & (row_f % FQ == 2 * c + j), c, j * H:(j + 1) * H] = 1.0
    both = np.concatenate([sel0, sel1, np.eye(P, dtype=np.float32)[:, None, :]], axis=1)
    return np.ascontiguousarray(both.reshape(P, -1))


def dlrm_tower(nc, dense, ids, tables, Wt1, bt1, Wt2, bt2, Wt3, W0, b0, W1, b1, consts, out):
    B, ND = dense.shape
    TILES = B // TB
    BG = B // P
    M1, M2 = Wt1.shape[1], Wt2.shape[1]
    K1, K2 = M1 // P, M2 // P
    NC = C0 + C1 // Q + 1

    PIECES = BG * Q
    x_dram = nc.dram_tensor("x_dram", (F, B, D), F32).ap()
    parts_dram = nc.dram_tensor("parts_dram", (Q, 2, FQ, B, D), F32).ap()

    everything = [(i, s) for i in range(TILES + 1) for s in slots_of(i, TILES)]

    def number(i, model, s, which=("pool", "vector")):
        chosen = [g for g in everything if SLOTS[g[1]][2] in which]
        per = sum(x[2] in which for x in SLOTS)
        at = chosen.index((model, s))
        return i * per + (at - model * per)

    def before(i, model, s, lag):
        at = everything.index((model, s)) - lag
        return at_group(i, model, at) if at >= 0 else None

    def at_group(i, model, at):
        mi, ms = everything[at]
        return i + (mi - model) if mi != model else i, mi, ms

    def last_user(i, model, s, buffer):
        for at in range(everything.index((model, s)) - 1, -1, -1):
            if buffer(*everything[at]) == buffer(model, s):
                return at_group(i, model, at)
        return None

    def last_in_banks(i, model, s):
        banks, found = set(banks_of(s)), []
        for at in range(everything.index((model, s)) - 1, -1, -1):
            if banks & set(banks_of(everything[at][1])):
                banks -= set(banks_of(everything[at][1]))
                found.append(at_group(i, model, at))
        return found

    def part_buffer(model, s):
        return PART_BUFFERS[model % NBUF * S + s]

    def z_buffer(model, s):
        return Z_BUFFERS[model % NBUF * len(POOL_SLOTS) + POOL_SLOTS.index(s)] if s in POOL_SLOTS else None

    with ExitStack() as ctx:
        def sb(name, shape, dt=F32):
            return ctx.enter_context(nc.sbuf_tensor(name, shape, dt))

        def pb(name, shape):
            return ctx.enter_context(nc.psum_tensor(name, shape, F32))

        def sem(name):
            return ctx.enter_context(nc.semaphore(name))

        idx = sb("idx", [P, BG, F], mybir.dt.int32)
        idx_now = sb("idx_now", [P, FQ], mybir.dt.int32)
        EMB = Q + AHEAD
        emb = sb("emb", [P, EMB, FQ, D])
        emb_hi = sb("emb_hi", [P, EMB, FQ, D], F32R)
        emb_lo = sb("emb_lo", [P, EMB, FQ, D], F32R)
        const = sb("const", [P, NC, P])
        sel = sb("sel", [P, NC - 1, P], F32R)
        ident = const[:, NC - 1, :]
        w0s = sb("w0s", [P, 20, F])
        w_hi = sb("w_hi", [P, C0 + C1, P], F32R)
        w_lo = sb("w_lo", [P, C0 + C1, P], F32R)
        b0_sb = sb("b0_sb", [P, 1])
        b1_sb = sb("b1_sb", [P, 1])
        x4 = sb("x4", [P, NBUF, N])
        parts = sb("parts", [P, NBUF, N], F32R)
        hid = sb("hid", [P, NBUF, N])
        z = sb("z", [P, ZRING, PAIR, N])
        z_hi = sb("z_hi", [P, RING, PAIR, N], F32R)
        z_lo = sb("z_lo", [P, RING, PAIR, N], F32R)
        z_flat = z[:, :, :, :].rearrange("p b k n -> p (b k n)")
        w0 = z_flat[:, 0:F * F]
        w1 = z_flat[:, F * F:F * F + H * F].rearrange("p (h m) -> p h m", m=F)
        w1s = hid[:, :, :].rearrange("p b n -> p (b n)").rearrange("p (m h) -> p m h", h=H)
        direct1 = sb("direct1", [P, N])
        dense_sb = sb("dense_sb", [P, BG, ND])
        zA = sb("zA", [P, B])
        zB = sb("zB", [P, B])
        wtA = sb("wtA", [P, M1])
        wtB = sb("wtB", [P, M1])
        wt2 = sb("wt2", [P, K1, M2])
        wt3 = sb("wt3", [P, K2])
        bt1_sb = sb("bt1_sb", [P, K1])
        bt2_sb = sb("bt2_sb", [P, K2])
        emb_flat = emb[:, :, :, :].rearrange("p e f d -> p (e f d)")
        h1 = emb_flat[:, 0:K1 * B].rearrange("p (k b) -> p k b", k=K1)
        h2 = emb_flat[:, K1 * B:(K1 + K2) * B].rearrange("p (k b) -> p k b", k=K2)
        y = sb("y", [1, B])

        spread = pb("spread", [P, BANKS, N])
        out0 = pb("out0", [P, N])
        out1 = pb("out1", [P, N])
        mlp3 = spread[0:1, BANKS - 1, :]
        WGROUP = 3
        WGROUPS = (C0 + C1) // WGROUP

        def w_bank(g):
            return spread[:, 2 * (g % 3), 0:WGROUP * P].rearrange("p (c n) -> p c n", n=P)

        def spread_of(s):
            return spread[:, SLOTS[s][3]:SLOTS[s][3] + len(SLOTS[s][1]), :]

        def mlp1(k):
            return spread[:, k, :]

        def mlp2(k):
            return (out0, out1)[k][:, :]

        idx_in = sem("idx_in")
        gathered = [sem(f"gathered{p}") for p in range(EMB)]
        cut_hi = sem("cut_hi")
        cut_lo = sem("cut_lo")
        stored = sem("stored")
        idx_copied = sem("idx_copied")
        loop_gathered = sem("loop_gathered")
        w_in = sem("w_in")
        c_in = sem("c_in")
        m_in = sem("m_in")
        dense_t_done = sem("dense_t_done")
        hid_done = sem("hid_done")
        zeroed = sem("zeroed")
        parts_zeroed = sem("parts_zeroed")
        sel_done = sem("sel_done")
        w0s_done = sem("w0s_done")
        w1s_done = sem("w1s_done")
        transposed = sem("transposed")
        w_hi_done = sem("w_hi_done")
        w_lo_done = sem("w_lo_done")
        rem_w_done = sem("rem_w_done")
        dense_done = sem("dense_done")
        x_in = [sem(f"x_in{k}") for k in range(NBUF)]
        spread_done = sem("spread_done")
        mult_done = sem("mult_done")
        hi_done = sem("hi_done")
        pool_lo_done = sem("pool_lo_done")
        dve_lo_done = sem("dve_lo_done")
        prod_done = sem("prod_done")
        direct0_done = sem("direct0_done")
        out1_read = sem("out1_read")
        sum0_done = sem("sum0_done")
        sum1_done = sem("sum1_done")
        m1_done = sem("m1_done")
        h1_done = sem("h1_done")
        m2_done = sem("m2_done")
        h2_done = sem("h2_done")
        m3_done = sem("m3_done")
        y_done = sem("y_done")
        y_out = sem("y_out")

        LOADS = 16 * (Q + Q)
        STORES = 16 * 3
        FIRST, LAST = 2, TILES - 2
        TURNS = (LAST - FIRST) // NBUF
        BUSY = PIECES - EMB
        assert (LAST - FIRST) % NBUF == 0 and BUSY % Q == Q - AHEAD and AHEAD == 2

        def iterations(eng, body):
            for i in range(FIRST):
                body(i, i, None)
            with eng.Fori(0, BUSY) as turn:
                for r in range(NBUF):
                    body(turn * NBUF + (FIRST + r), FIRST + NBUF + r, turn if r == NBUF - 1 else None)
            with eng.Fori(BUSY, TURNS) as turn:
                for r in range(NBUF):
                    body(turn * NBUF + (FIRST + r), FIRST + NBUF + r, None)
            for i in range(LAST, TILES + 1):
                body(i, i, None)

        def landed(i, model):
            first = model % NBUF
            return (i - (first - NBUF)) * (LOADS // NBUF)

        block = ctx.enter_context(nc.Block())

        @block.sync
        def _(sp):
            sp.dma_start(idx[:, :, :], ids.rearrange("(g p) f -> p g f", p=P)).then_inc(idx_in, 16)
            sp.dma_start(const[:, :, :], consts.rearrange("p (n m) -> p n m", m=P)).then_inc(c_in, 16)
            sp.dma_start(w0, W0).then_inc(w_in, 16)
            sp.dma_start(w1, W1.rearrange("o (h m) -> o h m", m=F)).then_inc(w_in, 16)
            sp.dma_start(b0_sb[:, :], b0.rearrange("(o a) -> o a", a=1)).then_inc(m_in, 16)
            sp.dma_start(b1_sb[:, :], b1.rearrange("(o a) -> o a", a=1)).then_inc(m_in, 16)
            sp.dma_start(dense_sb[:, :, :], dense.rearrange("(g p) n -> p g n", p=P)).then_inc(m_in, 16)
            sp.wait_ge(zeroed, 2)
            sp.dma_start(wtA[0:ND, :], Wt1[3 * H:3 * H + ND, :]).then_inc(m_in, 16)
            sp.dma_start(wtA[H:P, :], Wt1[0:H, :]).then_inc(m_in, 16)
            sp.dma_start(wtB[:, :], Wt1[H:3 * H, :]).then_inc(m_in, 16)
            sp.dma_start(wt2[:, :, :], Wt2.rearrange("(k p) n -> p k n", p=P)).then_inc(m_in, 16)
            sp.dma_start(wt3[:, :], Wt3.rearrange("(k p) n -> p (k n)", p=P), allow_slow_non_contiguous=True).then_inc(m_in, 16)
            sp.dma_start(bt1_sb[:, :], bt1.rearrange("(k p) -> p k", p=P), allow_slow_non_contiguous=True).then_inc(m_in, 16)
            sp.dma_start(bt2_sb[:, :], bt2.rearrange("(k p) -> p k", p=P), allow_slow_non_contiguous=True).then_inc(m_in, 16)
            def store_piece(e, g, q):
                rows, fields = bass.ds(g * P, P), bass.ds(q * FQ, FQ)
                sp.dma_start(x_dram[fields, rows, :].rearrange("f b d -> b f d"), emb[:, e, :, :]).then_inc(stored, 16)
                for part, src in enumerate((emb_hi, emb_lo)):
                    dst = parts_dram.rearrange("q r m b d -> (q r m) b d")[bass.ds(q * (2 * FQ) + part * FQ, FQ), rows, :]
                    sp.dma_start(dst.rearrange("m b d -> b m d"), src[:, e, :, :].bitcast(F32)).then_inc(stored, 16)

            def store_ahead(e):
                sp.wait_ge(cut_lo, e + 1)
                store_piece(e, e // Q, e % Q)

            x_cols = x_dram.rearrange("f b d -> f (b d)")
            p_cols = parts_dram.rearrange("q r m b d -> q (r m) (b d)")

            def load(i, model):
                buf = model % NBUF
                cols = bass.ds(i * N, N)
                for q in range(Q):
                    sp.dma_start(parts[q * 32:q * 32 + 2 * FQ, buf, :].bitcast(F32), p_cols[q, :, cols]).then_inc(x_in[buf], 16)
                for q in range(Q):
                    sp.dma_start(x4[q * 32:q * 32 + F, buf, :], x_cols[:, cols]).then_inc(x_in[buf], 16)

            for e in range(Q):
                store_ahead(e)
            sp.wait_ge(parts_zeroed, 1)
            sp.wait_ge(stored, STORES * Q)
            for i in range(NBUF):
                load(i, i)
            for e in range(Q, EMB):
                store_ahead(e)
            def body(i, model):
                sp.wait_ge(spread_done, number(i, model, LAST1) + 1)
                load(i + (NBUF - 1), model + NBUF - 1)

            body(1, 1)
            with sp.Fori(0, BUSY) as turn:
                piece = turn + EMB
                g, q = sp.snap(piece // Q), sp.snap(piece % Q)
                sp.wait_ge(stored, STORES * piece)
                for r in range(NBUF):
                    body(turn * NBUF + (FIRST + r), FIRST + NBUF + r)
                sp.wait_ge(cut_lo, piece + 1)
                store_piece(0, g, q)
            sp.wait_ge(stored, STORES * PIECES)
            with sp.Fori(BUSY, TURNS - 1) as turn:
                for r in range(NBUF):
                    body(turn * NBUF + (FIRST + r), FIRST + NBUF + r)
            for i in range(LAST - NBUF, TILES - NBUF + 1):
                body(i, i)

            sp.wait_ge(y_done, 1)
            sp.dma_start(out.rearrange("(a b) n -> a (b n)", a=1), y[:, :]).then_inc(y_out, 16)
            sp.wait_ge(y_out, 16)

        @block.gpsimd
        def _(pool):
            nc.gpsimd.memset(wtA[:, :], 0.0).then_inc(zeroed, 1)
            nc.gpsimd.memset(zA[:, :], 0.0).then_inc(zeroed, 1)
            pool.wait_ge(idx_in, 16)
            for e in range(EMB):
                for f in range(FQ):
                    field = e % Q * FQ + f
                    pool.indirect_dma_start(
                        emb[:, e, f, :], None, tables[field],
                        bass.IndirectOffsetOnAxis(ap=idx[:, e // Q, field:field + 1].bitcast(U32), axis=0),
                    ).then_inc(gathered[e], 16)

            def body(i, model, between=None):
                for s in slots_of(model, TILES):
                    if s in POOL_SLOTS:
                        pool.wait_ge(hi_done, number(i, model, s) + 1)
                        buf = part_buffer(model, s)
                        k = len(SLOTS[s][1])
                        nc.gpsimd.tensor_tensor(z_lo[:, buf, 0:k, :], z[:, z_buffer(model, s), 0:k, :],
                                                z_hi[:, buf, 0:k, :].bitcast(F32), ALU.subtract).then_inc(pool_lo_done, 1)
                        if between and POOL_SLOTS.index(s) in between:
                            between[POOL_SLOTS.index(s)]()

            def busy_turn(turn, k, g):
                q = (k + AHEAD) % Q

                def fetch_indices():
                    pool.wait_ge(stored, STORES * (turn + EMB))
                    nc.gpsimd.tensor_copy(idx_now[:, :], idx[:, g, q * FQ:(q + 1) * FQ]).then_inc(idx_copied, 1)
                    pool.wait_ge(idx_copied, turn + 1)

                def gather(f):
                    pool.indirect_dma_start(
                        emb[:, 0, f, :], None, tables[q * FQ + f],
                        bass.IndirectOffsetOnAxis(ap=idx_now[:, f:f + 1].bitcast(U32), axis=0),
                    ).then_inc(loop_gathered, 16)

                for r in range(NBUF):
                    between = {}
                    for n, after in enumerate(GATHERS[r]):
                        f = r * len(GATHERS[r]) + n
                        between[after] = lambda f=f: gather(f)
                    if r == 0:
                        between[GATHERS[0][0] - 1] = fetch_indices
                    body(turn * NBUF + (FIRST + r), FIRST + NBUF + r, between)

            for i in range(FIRST):
                body(i, i)
            with pool.Fori(0, BUSY // Q) as v:
                for k in range(Q):
                    busy_turn(v * Q + k, k, bass.ds(v + (1 + (k >= Q - AHEAD)), 1))
            for k in range(BUSY % Q):
                busy_turn(BUSY // Q * Q + k, k, BG - 1)
            with pool.Fori(BUSY, TURNS) as turn:
                for r in range(NBUF):
                    body(turn * NBUF + (FIRST + r), FIRST + NBUF + r)
            for i in range(LAST, TILES + 1):
                body(i, i)

        @block.scalar
        def _(act):
            act.wait_ge(w_in, 32)
            nc.scalar.activation(w1s.rearrange("p m h -> p h m"), w1, ACT.Copy).then_inc(w1s_done, 1)
            act.wait_ge(c_in, 16)
            nc.scalar.activation(sel[:, :, :], const[:, 0:NC - 1, :], ACT.Copy).then_inc(sel_done, 1)
            for g in range(WGROUPS):
                act.wait_ge(transposed, g + 1)
                nc.scalar.activation(w_hi[:, g * WGROUP:(g + 1) * WGROUP, :], w_bank(g), ACT.Copy).then_inc(w_hi_done, 1)

            def cut(e):
                nc.scalar.activation(emb_hi[:, e, :, :], emb[:, e, :, :], ACT.Copy).then_inc(cut_hi, 1)

            for e in range(Q):
                act.wait_ge(gathered[e], 16 * FQ)
                cut(e)
            act.wait_ge(m_in, 16 * 10)

            def read0(t, model):
                act.wait_ge(prod_done, number(t, model, LAST0) + 1)
                nc.scalar.activation(hid[:, model % NBUF, :], out0[:, :], ACT.Relu, bias=b0_sb[:, :]).then_inc(direct0_done, 1)

            def copy0(t, model):
                act.wait_ge(sum0_done, t + 1)
                nc.scalar.activation(hid[H:P, model % NBUF, :], out0[0:H, :], ACT.Relu, bias=b0_sb[0:H, :]).then_inc(hid_done, 1)

            def read1(t, model):
                act.wait_ge(prod_done, number(t + 1, model + 1, LAST1) + 1)
                if model > 0:
                    act.wait_ge(sum1_done, t)
                nc.scalar.activation(direct1[:, :], out1[:, :], ACT.Relu, bias=b1_sb[:, :]).then_inc(out1_read, 1)

            def sum1(t, model, row):
                if row == 0:
                    act.wait_ge(out1_read, t + 1)
                cols = direct1[:, row * D:(row + 1) * D]
                done = nc.scalar.activation(cols, cols, ACT.Copy, accum_out=zB[:, bass.ds(t * TB + row, 1)])
                if row == TB - 1:
                    done.then_inc(sum1_done, 1)

            def body(i, model, turn):
                for s in slots_of(model, TILES):
                    k, on_pool = len(SLOTS[s][1]), s in POOL_SLOTS
                    act.wait_ge(mult_done, number(i, model, s) + 1)
                    if (old := last_user(i, model, s, part_buffer)):
                        act.wait_ge(prod_done, number(*old) + 1)
                    src = z[:, z_buffer(model, s), 0:k, :] if on_pool else spread_of(s)
                    nc.scalar.activation(z_hi[:, part_buffer(model, s), 0:k, :], src, ACT.Copy).then_inc(hi_done, 1)
                    if (model, s) == (0, LAST0):
                        read0(i, model)
                        copy0(i, model)
                    for work, last, lag in ((read0, LAST0, READ0), (copy0, LAST0, COPY0), (read1, LAST1, READ1)):
                        t, t_model, t_slot = before(i, model, s, lag) or (0, 0, None)
                        if t_slot == last and t_model > 0:
                            work(*((t, t_model) if last == LAST0 else (t - 1, t_model - 1)))
                    for row in range(TB):
                        t, t_model, t_slot = before(i, model, s, SUM1 + row // 2) or (0, 0, None)
                        if t_slot == LAST1 and t_model > 0:
                            sum1(t - 1, t_model - 1, row)
                    if (model, s) == (1, 6):
                        for e in range(Q, EMB):
                            act.wait_ge(gathered[e], 16 * FQ)
                            cut(e)
                    if s == 6 and turn is not None:
                        act.wait_ge(loop_gathered, 16 * FQ * (turn + 1))
                        act.wait_ge(stored, STORES * (turn + EMB))
                        cut(0)

            iterations(act, body)
            for row in range(TB):
                if SUM1 + row // 2 > len(slots_of(TILES, TILES)):
                    sum1(TILES - 2, TILES - 2, row)
            read1(TILES - 1, TILES - 1)
            for row in range(TB):
                sum1(TILES - 1, TILES - 1, row)

            for k in range(K1):
                act.wait_ge(m1_done, k + 1)
                nc.scalar.activation(h1[:, k, :], mlp1(k), ACT.Relu, bias=bt1_sb[:, k:k + 1]).then_inc(h1_done, 1)
            for k in range(K2):
                act.wait_ge(m2_done, k + 1)
                nc.scalar.activation(h2[:, k, :], mlp2(k), ACT.Relu, bias=bt2_sb[:, k:k + 1]).then_inc(h2_done, 1)
            act.wait_ge(m3_done, 1)
            nc.scalar.activation(y[:, :], mlp3, ACT.Copy).then_inc(y_done, 1)

        @block.vector
        def _(dve):
            nc.vector.memset(parts[:, :, :].bitcast(F32), 0.0).then_inc(parts_zeroed, 1)
            dve.wait_ge(w_in, 32)
            step = F + 1

            def run(at, n):
                return w0[:, at:at + step * (n - 1) + 1:step]

            nc.vector.tensor_copy(w0s[:, 0, :], run(0, F))
            for s in range(1, F // 2):
                nc.vector.tensor_tensor(w0s[:, s, 0:F - s], run(s, F - s), run(F * s, F - s), ALU.add)
                nc.vector.tensor_tensor(w0s[:, s, F - s:F], run(F * (F - s), s), run(F - s, s), ALU.add)
            for r in range(4):
                nc.vector.tensor_copy(w0s[:, 16 + r, 0:F // 2], run(F // 2, F // 2))
                last = nc.vector.tensor_copy(w0s[:, 16 + r, F // 2:F], run(F * (F // 2), F // 2))
            last.then_inc(w0s_done, 1)

            for g in range(WGROUPS):
                dve.wait_ge(w_hi_done, g + 1)
                part = slice(g * WGROUP, (g + 1) * WGROUP)
                nc.vector.tensor_tensor(w_lo[:, part, :], w_bank(g), w_hi[:, part, :].bitcast(F32), ALU.subtract).then_inc(w_lo_done, 1)
            dve.wait_ge(w_lo_done, WGROUPS)
            for a in (F, 3 * F):
                last = nc.vector.tensor_copy(w_hi[a:a + F, C0 - 1, :], w_lo[a:a + F, C0 - 1, :])
            last.then_inc(rem_w_done, 1)
            dve.wait_ge(zeroed, 2)
            dve.wait_ge(dense_t_done, 1)
            nc.vector.tensor_copy(zA[0:ND, :], out0[0:ND, :]).then_inc(dense_done, 1)

            def cut(e, number):
                dve.wait_ge(cut_hi, number + 1)
                nc.vector.tensor_tensor(emb_lo[:, e, :, :], emb[:, e, :, :], emb_hi[:, e, :, :].bitcast(F32),
                                        ALU.subtract).then_inc(cut_lo, 1)

            for e in range(Q):
                cut(e, e)

            def low_parts(i, model, s):
                buf, src = part_buffer(model, s), spread_of(s)
                dve.wait_ge(hi_done, number(i, model, s) + 1)
                if SLOTS[s][1] == [C0 - 1]:
                    nc.vector.tensor_tensor(z_hi[H:P, buf, 0, :], src[H:P, 0, :], z_hi[H:P, buf, 0, :].bitcast(F32),
                                            ALU.subtract).then_inc(dve_lo_done, 1)
                else:
                    k = len(SLOTS[s][1])
                    nc.vector.tensor_tensor(z_lo[:, buf, 0:k, :], src, z_hi[:, buf, 0:k, :].bitcast(F32),
                                            ALU.subtract).then_inc(dve_lo_done, 1)

            def sum_over_d(dst, src, i, done):
                nc.vector.tensor_reduce(dst[:, bass.ds(i * TB, TB)], src.rearrange("p (b d) -> p b d", d=D),
                                        AX_X, ALU.add).then_inc(done, 1)

            def sum0(t, model):
                dve.wait_ge(direct0_done, t + 1)
                sum_over_d(zA[H:P, :], hid[H:P, model % NBUF, :], t, sum0_done)

            def body(i, model, turn):
                for s in slots_of(model, TILES):
                    layer, k = SLOTS[s][0], len(SLOTS[s][1])
                    dve.wait_ge(spread_done, number(i, model, s) + 1)
                    if s == FIRST0:
                        dve.wait_ge(x_in[model % NBUF], landed(i, model))
                    if s == FIRST1:
                        dve.wait_ge(hid_done, i)
                    dst = spread_of(s)
                    if s in POOL_SLOTS:
                        dst = z[:, z_buffer(model, s), 0:k, :]
                        if (old := last_user(i, model, s, z_buffer)):
                            dve.wait_ge(pool_lo_done, number(*old, ("pool",)) + 1)
                    factor = x4[:, model % NBUF, :] if layer == 0 else hid[:, (model - 1) % NBUF, :]
                    nc.vector.tensor_tensor(dst, spread_of(s),
                                            factor.unsqueeze(1).broadcast_to([P, k, N]), ALU.mult).then_inc(mult_done, 1)
                    old = before(i, model, s, 1)
                    if old and old[2] not in POOL_SLOTS and (model, s) != (1, 0):
                        low_parts(*old)
                    if (model, s) == (0, LAST0):
                        low_parts(i, model, s)
                    if (model, s) == (0, LAST0):
                        sum0(i, model)
                    t, t_model, t_slot = before(i, model, s, SUM0) or (0, 0, None)
                    if t_slot == LAST0 and t_model > 0:
                        sum0(t, t_model)
                    if (model, s) == (1, 8):
                        for e in range(Q, EMB):
                            cut(e, e)
                    if s == 8 and turn is not None:
                        cut(0, turn + EMB)

            iterations(dve, body)

        @block.tensor
        def _(pe):
            pe.wait_ge(c_in, 16)
            pe.wait_ge(w0s_done, 1)
            pe.wait_ge(w1s_done, 1)
            for g in range(WGROUPS):
                if g >= 3:
                    pe.wait_ge(w_lo_done, g - 2)
                for k in range(WGROUP):
                    c = g * WGROUP + k
                    src = w0s[:, 4 * c:4 * c + 4, :] if c < C0 else w1s[:, 2 * (c - C0):2 * (c - C0) + 2, :]
                    last = nc.tensor.transpose(w_bank(g)[:, k, :], src, ident)
                last.then_inc(transposed, 1)
            pe.wait_ge(m_in, 16 * 10)
            for g in range(BG):
                last = nc.tensor.transpose(out0[0:ND, g * P:(g + 1) * P], dense_sb[:, g, :], ident)
            last.then_inc(dense_t_done, 1)
            pe.wait_ge(sel_done, 1)
            pe.wait_ge(rem_w_done, 1)
            pe.wait_ge(dense_done, 1)

            def spread_group(i, model, s):
                layer, chunks, _, _ = SLOTS[s]
                if s == FIRST0:
                    pe.wait_ge(x_in[model % NBUF], landed(i, model))
                for old in last_in_banks(i, model, s):
                    if old[2] in POOL_SLOTS:
                        pe.wait_ge(mult_done, number(*old) + 1)
                    else:
                        pe.wait_ge(dve_lo_done, number(*old, ("vector",)) + 1)
                for at, c in enumerate(chunks):
                    if layer == 0:
                        w, x = sel[:, c, :], parts[:, model % NBUF, :]
                    else:
                        q, buf = c // (C1 // Q), (model - 1) % NBUF
                        w, x = sel[32 * q:32 * q + 32, C0 + c % (C1 // Q), :], parts[32 * q:32 * q + 32, buf, :]
                    last = nc.tensor.matmul(spread_of(s)[:, at, :], w, x, start=True, stop=True)
                last.then_inc(spread_done, 1)

            def products(i, model, s):
                layer, chunks, kind, _ = SLOTS[s]
                buf, base, out_bank = part_buffer(model, s), (0, C0)[layer], (out0, out1)[layer]
                if s == FIRST0 and model > 0:
                    pe.wait_ge(hid_done, i)
                if s == FIRST1 and model > 1:
                    pe.wait_ge(out1_read, i - 1)
                pe.wait_ge(pool_lo_done if kind == "pool" else dve_lo_done, number(i, model, s, (kind,)) + 1)
                passes = []
                for at, c in enumerate(chunks):
                    passes.append((w_hi[:, base + c, :], z_hi[:, buf, at, :]))
                    if not (layer == 0 and c == C0 - 1):
                        passes.append((w_lo[:, base + c, :], z_hi[:, buf, at, :]))
                        passes.append((w_hi[:, base + c, :], z_lo[:, buf, at, :]))
                for m, (w, x) in enumerate(passes):
                    last = nc.tensor.matmul(out_bank[:, :], w, x, start=(s in (FIRST0, FIRST1) and m == 0),
                                            stop=(s in (LAST0, LAST1) and m == len(passes) - 1))
                last.then_inc(prod_done, 1)

            def body(i, model, turn):
                for s in slots_of(model, TILES):
                    spread_group(i, model, s)
                    if (old := before(i, model, s, LAG)) and old[1] > 0:
                        products(*old)
                if model == 0:
                    for s in slots_of(model, TILES):
                        products(i, model, s)

            iterations(pe, body)
            for _, s in everything[-LAG:]:
                products(TILES, TILES, s)

            pe.wait_ge(sum0_done, TILES)
            pe.wait_ge(sum1_done, TILES)
            for k in range(K1):
                nc.tensor.matmul(mlp1(k), wtA[:, k * P:(k + 1) * P], zA[:, :], start=True, stop=False)
                nc.tensor.matmul(mlp1(k), wtB[:, k * P:(k + 1) * P], zB[:, :], start=False, stop=True).then_inc(m1_done, 1)
            for j in range(K2):
                for k in range(K1):
                    pe.wait_ge(h1_done, k + 1)
                    last = nc.tensor.matmul(mlp2(j), wt2[:, k, j * P:(j + 1) * P], h1[:, k, :], start=(k == 0), stop=(k == K1 - 1))
                last.then_inc(m2_done, 1)
            for k in range(K2):
                pe.wait_ge(h2_done, k + 1)
                last = nc.tensor.matmul(mlp3, wt3[:, k:k + 1], h2[:, k, :], start=(k == 0), stop=(k == K2 - 1))
            last.then_inc(m3_done, 1)


_INS = (["dense_ctx", "ids"] + [f"tbl_{f}" for f in range(F)]
        + ["W_top1", "b_top1", "W_top2", "b_top2", "W_top3", "L0_rec_W0", "L0_rec_b0", "L0_rec_W1", "L0_rec_b1"])


def kernel(**inputs):
    import numpy as _np
    import concourse.bacc as _bacc
    from concourse import mybir as _mybir
    from concourse.bass_utils import run_bass_kernel_spmd as _run

    nc = _bacc.Bacc("TRN2", target_bir_lowering=False, num_devices=1)
    arrays, aps = {}, []
    for name in _INS:
        a = _np.ascontiguousarray(inputs[name])
        arrays[f"in_{name}"] = a
        aps.append(nc.dram_tensor(f"in_{name}", a.shape, _mybir.dt.from_np(a.dtype), kind="ExternalInput").ap())
    c = constants()
    arrays["in_constants"] = c
    c_ap = nc.dram_tensor("in_constants", c.shape, _mybir.dt.from_np(c.dtype), kind="ExternalInput").ap()
    out = nc.dram_tensor("out", (inputs["ids"].shape[0], 1), _mybir.dt.float32, kind="ExternalOutput").ap()
    dlrm_tower(nc, aps[0], aps[1], aps[2:2 + F], *aps[2 + F:], c_ap, out)
    r = _run(nc, [arrays], core_ids=[0])
    return r.results[0]["out"]
```

```python
from contextlib import ExitStack

import numpy as np

import concourse.bass as bass
from concourse import mybir

ALU = mybir.AluOpType
ACT = mybir.ActivationFunctionType
AX_X = mybir.AxisListType.X
F32 = mybir.dt.float32
F32R = mybir.dt.float32r
U32 = mybir.dt.uint32

P = 128
F = 32
D = 64
O = 128
H = O // 2
TB = 8
N = TB * D
Q = 4
FQ = F // Q
C0 = 5
C1 = H * F // P
NBUF = 4
PAIR = 2
BANKS = 6
RING = 8
ZRING = 4
LAG = 6
READ0, SUM0, COPY0 = 6, 7, 7
READ1, SUM1 = 6, 7
INDEX_SLOT, GATHER_SLOTS, HI_SLOT, LO_SLOT = 1, (2, 4), 10, 11
FIRST_CUT_SLOT = 5

ORDER1 = [(n % Q) * (C1 // Q) + n // Q for n in range(C1)]
SLOTS = [
    (0, [4], "vector", 5), (0, [0, 1], "pool", 2), (1, ORDER1[0:2], "pool", 0), (1, ORDER1[2:4], "vector", 2),
    (0, [2, 3], "pool", 4), (1, ORDER1[4:5], "pool", 1), (1, ORDER1[5:6], "vector", 3),
    (1, ORDER1[6:8], "vector", 4), (1, ORDER1[8:10], "pool", 0), (1, ORDER1[10:12], "vector", 2),
    (1, ORDER1[12:14], "pool", 4), (1, ORDER1[14:16], "pool", 0),
]
S = len(SLOTS)
FIRST0, LAST0, FIRST1, LAST1 = 0, 4, 2, S - 1
POOL_SLOTS = [s for s in range(S) if SLOTS[s][2] == "pool"]


def rounds(total, most):
    short = -total % most
    full = (total - short * (most - 1)) // most
    assert full * most + short * (most - 1) == total and full >= 0
    return [b for r in range(full + short) for b in range(most if r < full else most - 1)]


PART_BUFFERS = rounds(NBUF * S, RING)
Z_BUFFERS = rounds(NBUF * len(POOL_SLOTS), ZRING)


def banks_of(s):
    return range(SLOTS[s][3], SLOTS[s][3] + len(SLOTS[s][1]))


def slots_of(i, tiles):
    return [s for s in range(S) if (i > 0 if SLOTS[s][0] else i < tiles)]


def constants():
    row_f = np.full(P, -1)
    for q in range(Q):
        for part in range(2):
            for m in range(FQ):
                row_f[q * 32 + part * FQ + m] = q * FQ + m
    sel0 = np.zeros((P, C0, P), np.float32)
    for k in range(C0):
        for g in range(4):
            for i in range(F):
                shift = 16 if k == 4 else 4 * k + g
                sel0[row_f == (i + shift) % F, k, g * F + i] = 1.0
    sel1 = np.zeros((P, C1 // Q, P), np.float32)
    for c in range(C1 // Q):
        for j in range(2):
            sel1[(row_f >= 0) & (row_f % FQ == 2 * c + j), c, j * H:(j + 1) * H] = 1.0
    both = np.concatenate([sel0, sel1, np.eye(P, dtype=np.float32)[:, None, :]], axis=1)
    return np.ascontiguousarray(both.reshape(P, -1))


def dlrm_tower(nc, dense, ids, offsets, table, Wt1, bt1, Wt2, bt2, Wt3, W0, b0, W1, b1, consts, out):
    B, ND = dense.shape
    TILES = B // TB
    BG = B // P
    M1, M2 = Wt1.shape[1], Wt2.shape[1]
    K1, K2 = M1 // P, M2 // P
    NC = C0 + C1 // Q + 1
    GJ = TB * F // P

    x_dram = nc.dram_tensor("x_dram", (F, B, D), F32).ap()
    parts_dram = nc.dram_tensor("parts_dram", (2, F, B, D), F32).ap()

    everything = [(i, s) for i in range(TILES + 1) for s in slots_of(i, TILES)]

    def number(i, model, s, which=("pool", "vector")):
        chosen = [g for g in everything if SLOTS[g[1]][2] in which]
        per = sum(x[2] in which for x in SLOTS)
        at = chosen.index((model, s))
        return i * per + (at - model * per)

    def before(i, model, s, lag):
        at = everything.index((model, s)) - lag
        return at_group(i, model, at) if at >= 0 else None

    def at_group(i, model, at):
        mi, ms = everything[at]
        return i + (mi - model) if mi != model else i, mi, ms

    def last_user(i, model, s, buffer):
        for at in range(everything.index((model, s)) - 1, -1, -1):
            if buffer(*everything[at]) == buffer(model, s):
                return at_group(i, model, at)
        return None

    def last_in_banks(i, model, s):
        banks, found = set(banks_of(s)), []
        for at in range(everything.index((model, s)) - 1, -1, -1):
            if banks & set(banks_of(everything[at][1])):
                banks -= set(banks_of(everything[at][1]))
                found.append(at_group(i, model, at))
        return found

    def place(model, s, slots):
        here = [x for x in slots_of(model, TILES) if x in slots]
        at = here.index(s) + (len(slots) - len(here) if model == 0 else 0)
        return model % NBUF * len(slots) + at

    def part_buffer(model, s):
        return PART_BUFFERS[place(model, s, range(S))]

    def z_buffer(model, s):
        return Z_BUFFERS[place(model, s, POOL_SLOTS)] if s in POOL_SLOTS else None

    with ExitStack() as ctx:
        def sb(name, shape, dt=F32):
            return ctx.enter_context(nc.sbuf_tensor(name, shape, dt))

        def pb(name, shape):
            return ctx.enter_context(nc.psum_tensor(name, shape, F32))

        def sem(name):
            return ctx.enter_context(nc.semaphore(name))

        idx = sb("idx", [P, TILES * GJ], mybir.dt.int32)
        off = sb("off", [P, 1], mybir.dt.int32)
        idx_now = sb("idx_now", [P, GJ], mybir.dt.int32)
        emb = sb("emb", [P, NBUF, GJ, D])
        emb_hi = sb("emb_hi", [P, NBUF, GJ, D], F32R)
        emb_lo = sb("emb_lo", [P, NBUF, GJ, D], F32R)
        const = sb("const", [P, NC, P])
        sel = sb("sel", [P, NC - 1, P], F32R)
        ident = const[:, NC - 1, :]
        w0s = sb("w0s", [P, 20, F])
        w_hi = sb("w_hi", [P, C0 + C1, P], F32R)
        w_lo = sb("w_lo", [P, C0 + C1, P], F32R)
        b0_sb = sb("b0_sb", [P, 1])
        b1_sb = sb("b1_sb", [P, 1])
        x4 = sb("x4", [P, NBUF, N])
        parts = sb("parts", [P, NBUF, N], F32R)
        hid = sb("hid", [P, NBUF, N])
        z = sb("z", [P, ZRING, PAIR, N])
        z_hi = sb("z_hi", [P, RING, PAIR, N], F32R)
        z_lo = sb("z_lo", [P, RING, PAIR, N], F32R)
        z_flat = z[:, :, :, :].rearrange("p b k n -> p (b k n)")
        w0 = z_flat[:, 0:F * F]
        w1 = z_flat[:, F * F:F * F + H * F].rearrange("p (h m) -> p h m", m=F)
        w1s = hid[:, :, :].rearrange("p b n -> p (b n)").rearrange("p (m h) -> p m h", h=H)
        direct1 = sb("direct1", [P, N])
        dense_sb = sb("dense_sb", [P, BG, ND])
        zA = sb("zA", [P, B])
        zB = sb("zB", [P, B])
        wtA = sb("wtA", [P, M1])
        wtB = sb("wtB", [P, M1])
        wt2 = sb("wt2", [P, K1, M2])
        wt3 = sb("wt3", [P, K2])
        bt1_sb = sb("bt1_sb", [P, K1])
        bt2_sb = sb("bt2_sb", [P, K2])
        h1 = z_flat[:, 0:K1 * B].rearrange("p (k b) -> p k b", k=K1)
        h2 = z_flat[:, K1 * B:(K1 + K2) * B].rearrange("p (k b) -> p k b", k=K2)
        y = sb("y", [1, B])

        spread = pb("spread", [P, BANKS, N])
        out0 = pb("out0", [P, N])
        out1 = pb("out1", [P, N])
        mlp3 = spread[0:1, BANKS - 1, :]
        WGROUP = 3
        WGROUPS = (C0 + C1) // WGROUP

        def w_bank(g):
            return spread[:, 2 * (g % 3), 0:WGROUP * P].rearrange("p (c n) -> p c n", n=P)

        def spread_of(s):
            return spread[:, SLOTS[s][3]:SLOTS[s][3] + len(SLOTS[s][1]), :]

        def mlp1(k):
            return spread[:, k, :]

        def mlp2(k):
            return (out0, out1)[k][:, :]

        idx_in = sem("idx_in")
        gathered = [sem(f"gathered{k}") for k in range(NBUF)]
        cut_hi = sem("cut_hi")
        cut_lo = sem("cut_lo")
        stored = [sem(f"stored{k}") for k in range(NBUF)]
        idx_ready = sem("idx_ready")
        idx_copied = sem("idx_copied")
        w_in = sem("w_in")
        w1_in = sem("w1_in")
        c_in = sem("c_in")
        b_in = sem("b_in")
        m_in = sem("m_in")
        dense_t_done = sem("dense_t_done")
        hid_done = sem("hid_done")
        zeroed = sem("zeroed")
        parts_zeroed = sem("parts_zeroed")
        sel_done = sem("sel_done")
        w0s_done = sem("w0s_done")
        w1s_done = sem("w1s_done")
        transposed = sem("transposed")
        w_hi_done = sem("w_hi_done")
        w_lo_done = sem("w_lo_done")
        rem_w_done = sem("rem_w_done")
        dense_done = sem("dense_done")
        x_in = [sem(f"x_in{k}") for k in range(NBUF)]
        spread_done = sem("spread_done")
        mult_done = sem("mult_done")
        hi_done = sem("hi_done")
        pool_lo_done = sem("pool_lo_done")
        dve_lo_done = sem("dve_lo_done")
        prod_done = sem("prod_done")
        direct0_done = sem("direct0_done")
        out1_read = sem("out1_read")
        sum0_done = sem("sum0_done")
        sum1_done = sem("sum1_done")
        m1_done = sem("m1_done")
        h1_done = sem("h1_done")
        m2_done = sem("m2_done")
        h2_done = sem("h2_done")
        m3_done = sem("m3_done")
        y_done = sem("y_done")
        y_out = sem("y_out")

        LOADS = 16 * (Q + 1)
        STORES = 16 * 3
        GATHERS = 16 * GJ
        FIRST, LAST = 2, TILES - NBUF - 2
        TURNS = (LAST - FIRST) // NBUF
        assert (LAST - FIRST) % NBUF == 0

        def iterations(eng, body):
            for i in range(FIRST):
                body(i, i)
            with eng.Fori(0, TURNS) as turn:
                for r in range(NBUF):
                    body(turn * NBUF + (FIRST + r), FIRST + NBUF + r)
            for i in range(LAST, TILES + 1):
                body(i, i)

        def landed(i, model, each):
            first = model % NBUF
            return (i - (first - NBUF)) * (each // NBUF)

        block = ctx.enter_context(nc.Block())

        @block.sync
        def _(sp):
            sp.dma_start(idx[:, :], ids).then_inc(idx_in, 16)
            sp.dma_start(off[:, :], offsets).then_inc(idx_in, 16)
            sp.dma_start(w0, W0).then_inc(w_in, 16)
            sp.dma_start(const[:, :, :], consts.rearrange("p (n m) -> p n m", m=P)).then_inc(c_in, 16)
            sp.dma_start(w1, W1.rearrange("o (h m) -> o h m", m=F)).then_inc(w1_in, 16)

            def store(t, model):
                buf, rows = model % NBUF, bass.ds(t * TB, TB)
                sp.wait_ge(cut_lo, t + 1)
                for src, dst in ((emb, x_dram), (emb_hi, parts_dram[0]), (emb_lo, parts_dram[1])):
                    src = src[:, buf, :, :] if src is emb else src[:, buf, :, :].bitcast(F32)
                    dst = dst[:, rows, :].rearrange("f (b j) d -> b f (j d)", j=GJ)
                    sp.dma_start(dst, src.rearrange("p j d -> p (j d)")).then_inc(stored[buf], 16)

            x_cols = x_dram.rearrange("f b d -> f (b d)")
            p_cols = parts_dram.rearrange("r (q m) b d -> q r m (b d)", q=Q)

            def load(t, model):
                buf, cols = model % NBUF, bass.ds(t * N, N)
                sp.wait_ge(stored[buf], landed(t, model, STORES))
                for q in range(Q):
                    sp.dma_start(parts[q * 32:q * 32 + 2 * FQ, buf, :].bitcast(F32), p_cols[q, :, :, cols]).then_inc(x_in[buf], 16)
                sp.dma_start(x4[:, buf, :], x_cols[:, cols].unsqueeze(0).broadcast_to([Q, F, N])).then_inc(x_in[buf], 16)

            store(0, 0)
            store(1, 1)
            sp.wait_ge(parts_zeroed, 1)
            load(0, 0)
            load(1, 1)
            store(2, 2)
            store(3, 3)
            load(2, 2)

            sp.wait_ge(zeroed, 2)
            sp.dma_start(wtA[0:ND, :], Wt1[3 * H:3 * H + ND, :]).then_inc(m_in, 16)
            sp.dma_start(wtA[H:P, :], Wt1[0:H, :]).then_inc(m_in, 16)
            sp.dma_start(wtB[:, :], Wt1[H:3 * H, :]).then_inc(m_in, 16)
            sp.dma_start(wt2[:, :, :], Wt2.rearrange("(k p) n -> p k n", p=P)).then_inc(m_in, 16)
            sp.dma_start(wt3[:, :], Wt3.rearrange("(k p) n -> p (k n)", p=P), allow_slow_non_contiguous=True).then_inc(m_in, 16)
            sp.dma_start(bt1_sb[:, :], bt1.rearrange("(k p) -> p k", p=P), allow_slow_non_contiguous=True).then_inc(m_in, 16)
            sp.dma_start(bt2_sb[:, :], bt2.rearrange("(k p) -> p k", p=P), allow_slow_non_contiguous=True).then_inc(m_in, 16)

            def body(i, model):
                if model + NBUF < TILES:
                    store(i + NBUF, model + NBUF)
                if model + NBUF - 1 < TILES:
                    sp.wait_ge(spread_done, number(i, model, slots_of(model, TILES)[-1]) + 1)
                    load(i + (NBUF - 1), model + NBUF - 1)

            iterations(sp, body)

            sp.wait_ge(y_done, 1)
            sp.dma_start(out.rearrange("(a b) n -> a (b n)", a=1), y[:, :]).then_inc(y_out, 16)
            sp.wait_ge(y_out, 16)

        @block.gpsimd
        def _(pool):
            nc.gpsimd.memset(wtA[:, :], 0.0).then_inc(zeroed, 1)
            nc.gpsimd.memset(zA[:, :], 0.0).then_inc(zeroed, 1)
            pool.wait_ge(idx_ready, 1)

            def gather(indices, buf, j):
                pool.indirect_dma_start(
                    emb[:, buf, j, :], None, table,
                    bass.IndirectOffsetOnAxis(ap=indices.bitcast(U32), axis=0),
                ).then_inc(gathered[buf], 16)

            for t in range(NBUF):
                for j in range(GJ):
                    gather(idx[:, t * GJ + j:t * GJ + j + 1], t, j)

            def body(i, model):
                buf = model % NBUF
                for s in slots_of(model, TILES):
                    if s in POOL_SLOTS:
                        pool.wait_ge(hi_done, number(i, model, s) + 1)
                        at, k = part_buffer(model, s), len(SLOTS[s][1])
                        nc.gpsimd.tensor_tensor(z_lo[:, at, 0:k, :], z[:, z_buffer(model, s), 0:k, :],
                                                z_hi[:, at, 0:k, :].bitcast(F32), ALU.subtract).then_inc(pool_lo_done, 1)
                    if model + NBUF < TILES:
                        if s == INDEX_SLOT:
                            pool.wait_ge(gathered[(model - 1) % NBUF], landed(i + (NBUF - 1), model + NBUF - 1, GATHERS))
                            pool.wait_ge(stored[buf], landed(i, model, STORES))
                            nc.gpsimd.tensor_copy(idx_now[:, :], idx[:, bass.ds((i + NBUF) * GJ, GJ)]).then_inc(idx_copied, 1)
                            pool.wait_ge(idx_copied, i + 1)
                        for j in range(GJ):
                            if s == (GATHER_SLOTS[j] if model else LAST0):
                                gather(idx_now[:, j:j + 1], buf, j)

            iterations(pool, body)

        @block.scalar
        def _(act):
            act.dma_start(b0_sb[:, :], b0.rearrange("(o a) -> o a", a=1)).then_inc(b_in, 16)
            act.dma_start(b1_sb[:, :], b1.rearrange("(o a) -> o a", a=1)).then_inc(b_in, 16)
            act.dma_start(dense_sb[:, :, :], dense.rearrange("(g p) n -> p g n", p=P)).then_inc(b_in, 16)

            def cut(t, model):
                buf = model % NBUF
                act.wait_ge(gathered[buf], landed(t, model, GATHERS))
                if model >= NBUF:
                    act.wait_ge(stored[buf], landed(t - NBUF, model - NBUF, STORES))
                nc.scalar.activation(emb_hi[:, buf, :, :], emb[:, buf, :, :], ACT.Copy).then_inc(cut_hi, 1)

            cut(0, 0)
            cut(1, 1)
            act.wait_ge(c_in, 16)
            nc.scalar.activation(sel[:, :, :], const[:, 0:NC - 1, :], ACT.Copy).then_inc(sel_done, 1)
            act.wait_ge(w1_in, 16)
            nc.scalar.activation(w1s.rearrange("p m h -> p h m"), w1, ACT.Copy).then_inc(w1s_done, 1)
            for g in range(WGROUPS):
                act.wait_ge(transposed, g + 1)
                nc.scalar.activation(w_hi[:, g * WGROUP:(g + 1) * WGROUP, :], w_bank(g), ACT.Copy).then_inc(w_hi_done, 1)

            for t in range(2, NBUF):
                cut(t, t)
            act.wait_ge(b_in, 16 * 3)

            def read0(t, model):
                act.wait_ge(prod_done, number(t, model, LAST0) + 1)
                nc.scalar.activation(hid[:, model % NBUF, :], out0[:, :], ACT.Relu, bias=b0_sb[:, :]).then_inc(direct0_done, 1)

            def copy0(t, model):
                act.wait_ge(sum0_done, t + 1)
                nc.scalar.activation(hid[H:P, model % NBUF, :], out0[0:H, :], ACT.Relu, bias=b0_sb[0:H, :]).then_inc(hid_done, 1)

            def read1(t, model):
                act.wait_ge(prod_done, number(t + 1, model + 1, LAST1) + 1)
                if model > 0:
                    act.wait_ge(sum1_done, t)
                nc.scalar.activation(direct1[:, :], out1[:, :], ACT.Relu, bias=b1_sb[:, :]).then_inc(out1_read, 1)

            def sum1(t, model, row):
                if row == 0:
                    act.wait_ge(out1_read, t + 1)
                cols = direct1[:, row * D:(row + 1) * D]
                done = nc.scalar.activation(cols, cols, ACT.Copy, accum_out=zB[:, bass.ds(t * TB + row, 1)])
                if row == TB - 1:
                    done.then_inc(sum1_done, 1)

            def body(i, model):
                for s in slots_of(model, TILES):
                    k, on_pool = len(SLOTS[s][1]), s in POOL_SLOTS
                    act.wait_ge(mult_done, number(i, model, s) + 1)
                    if (old := last_user(i, model, s, part_buffer)):
                        act.wait_ge(prod_done, number(*old) + 1)
                    src = z[:, z_buffer(model, s), 0:k, :] if on_pool else spread_of(s)
                    nc.scalar.activation(z_hi[:, part_buffer(model, s), 0:k, :], src, ACT.Copy).then_inc(hi_done, 1)
                    if (model, s) == (1, FIRST1 - 1):
                        read0(0, 0)
                        copy0(0, 0)
                    if (model, s) == (1, FIRST_CUT_SLOT):
                        cut(NBUF, NBUF)
                    for work, last, lag in ((read0, LAST0, READ0), (copy0, LAST0, COPY0), (read1, LAST1, READ1)):
                        t, t_model, t_slot = before(i, model, s, lag) or (0, 0, None)
                        if t_slot == last and t_model > 0:
                            work(*((t, t_model) if last == LAST0 else (t - 1, t_model - 1)))
                    for row in range(TB):
                        t, t_model, t_slot = before(i, model, s, SUM1 + row // 2) or (0, 0, None)
                        if t_slot == LAST1 and t_model > 0:
                            sum1(t - 1, t_model - 1, row)
                    if 0 < model < TILES - NBUF and s == HI_SLOT:
                        cut(i + NBUF, model + NBUF)

            iterations(act, body)
            for row in range(TB):
                if SUM1 + row // 2 > len(slots_of(TILES, TILES)):
                    sum1(TILES - 2, TILES - 2, row)
            read1(TILES - 1, TILES - 1)
            for row in range(TB):
                sum1(TILES - 1, TILES - 1, row)

            act.wait_ge(m_in, 16 * 7)
            for k in range(K1):
                act.wait_ge(m1_done, k + 1)
                nc.scalar.activation(h1[:, k, :], mlp1(k), ACT.Relu, bias=bt1_sb[:, k:k + 1]).then_inc(h1_done, 1)
            for k in range(K2):
                act.wait_ge(m2_done, k + 1)
                nc.scalar.activation(h2[:, k, :], mlp2(k), ACT.Relu, bias=bt2_sb[:, k:k + 1]).then_inc(h2_done, 1)
            act.wait_ge(m3_done, 1)
            nc.scalar.activation(y[:, :], mlp3, ACT.Copy).then_inc(y_done, 1)

        @block.vector
        def _(dve):
            dve.wait_ge(idx_in, 32)
            nc.vector.tensor_tensor(idx[:, :], idx[:, :], off[:, 0:1].broadcast_to([P, TILES * GJ]), ALU.add).then_inc(idx_ready, 1)
            nc.vector.memset(parts[:, :, :].bitcast(F32), 0.0).then_inc(parts_zeroed, 1)
            dve.wait_ge(w_in, 16)
            step = F + 1

            def run(at, n):
                return w0[:, at:at + step * (n - 1) + 1:step]

            nc.vector.tensor_copy(w0s[:, 0, :], run(0, F))
            for s in range(1, F // 2):
                nc.vector.tensor_tensor(w0s[:, s, 0:F - s], run(s, F - s), run(F * s, F - s), ALU.add)
                nc.vector.tensor_tensor(w0s[:, s, F - s:F], run(F * (F - s), s), run(F - s, s), ALU.add)
            for r in range(4):
                nc.vector.tensor_copy(w0s[:, 16 + r, 0:F // 2], run(F // 2, F // 2))
                last = nc.vector.tensor_copy(w0s[:, 16 + r, F // 2:F], run(F * (F // 2), F // 2))
            last.then_inc(w0s_done, 1)

            def cut(t, model):
                buf = model % NBUF
                dve.wait_ge(cut_hi, t + 1)
                nc.vector.tensor_tensor(emb_lo[:, buf, :, :], emb[:, buf, :, :], emb_hi[:, buf, :, :].bitcast(F32),
                                        ALU.subtract).then_inc(cut_lo, 1)

            cut(0, 0)
            cut(1, 1)
            for g in range(WGROUPS):
                dve.wait_ge(w_hi_done, g + 1)
                part = slice(g * WGROUP, (g + 1) * WGROUP)
                nc.vector.tensor_tensor(w_lo[:, part, :], w_bank(g), w_hi[:, part, :].bitcast(F32), ALU.subtract).then_inc(w_lo_done, 1)
            dve.wait_ge(w_lo_done, WGROUPS)
            for a in (F, 3 * F):
                last = nc.vector.tensor_copy(w_hi[a:a + F, C0 - 1, :], w_lo[a:a + F, C0 - 1, :])
            last.then_inc(rem_w_done, 1)

            for t in range(2, NBUF):
                cut(t, t)

            def low_parts(i, model, s):
                buf, src = part_buffer(model, s), spread_of(s)
                dve.wait_ge(hi_done, number(i, model, s) + 1)
                if SLOTS[s][1] == [C0 - 1]:
                    nc.vector.tensor_tensor(z_hi[H:P, buf, 0, :], src[H:P, 0, :], z_hi[H:P, buf, 0, :].bitcast(F32),
                                            ALU.subtract).then_inc(dve_lo_done, 1)
                else:
                    k = len(SLOTS[s][1])
                    nc.vector.tensor_tensor(z_lo[:, buf, 0:k, :], src, z_hi[:, buf, 0:k, :].bitcast(F32),
                                            ALU.subtract).then_inc(dve_lo_done, 1)

            def sum_over_d(dst, src, i, done):
                nc.vector.tensor_reduce(dst[:, bass.ds(i * TB, TB)], src.rearrange("p (b d) -> p b d", d=D),
                                        AX_X, ALU.add).then_inc(done, 1)

            def sum0(t, model):
                dve.wait_ge(direct0_done, t + 1)
                sum_over_d(zA[H:P, :], hid[H:P, model % NBUF, :], t, sum0_done)

            def body(i, model):
                for s in slots_of(model, TILES):
                    layer, k = SLOTS[s][0], len(SLOTS[s][1])
                    dve.wait_ge(spread_done, number(i, model, s) + 1)
                    if s == FIRST0:
                        dve.wait_ge(x_in[model % NBUF], landed(i, model, LOADS))
                    if s == FIRST1:
                        dve.wait_ge(hid_done, i)
                    dst = spread_of(s)
                    if s in POOL_SLOTS:
                        dst = z[:, z_buffer(model, s), 0:k, :]
                        if (old := last_user(i, model, s, z_buffer)):
                            dve.wait_ge(pool_lo_done, number(*old, ("pool",)) + 1)
                    factor = x4[:, model % NBUF, :] if layer == 0 else hid[:, (model - 1) % NBUF, :]
                    nc.vector.tensor_tensor(dst, spread_of(s),
                                            factor.unsqueeze(1).broadcast_to([P, k, N]), ALU.mult).then_inc(mult_done, 1)
                    if (model, s) == (0, LAST0):
                        dve.wait_ge(zeroed, 2)
                        dve.wait_ge(dense_t_done, 1)
                        nc.vector.tensor_copy(zA[0:ND, :], out0[0:ND, :]).then_inc(dense_done, 1)
                    old = before(i, model, s, 1)
                    if old and old[2] not in POOL_SLOTS and (model, s) != (1, 0):
                        low_parts(*old)
                    if (model, s) == (0, LAST0) and s not in POOL_SLOTS:
                        low_parts(i, model, s)
                    if (model, s) == (1, FIRST1 - 1):
                        sum0(0, 0)
                    if (model, s) == (1, FIRST_CUT_SLOT):
                        cut(NBUF, NBUF)
                    t, t_model, t_slot = before(i, model, s, SUM0) or (0, 0, None)
                    if t_slot == LAST0 and t_model > 0:
                        sum0(t, t_model)
                    if 0 < model < TILES - NBUF and s == LO_SLOT:
                        cut(i + NBUF, model + NBUF)

            iterations(dve, body)

        @block.tensor
        def _(pe):
            pe.wait_ge(c_in, 16)
            pe.wait_ge(w0s_done, 1)
            for g in range(WGROUPS):
                if g >= 3:
                    pe.wait_ge(w_lo_done, g - 2)
                if g == C0 // WGROUP:
                    pe.wait_ge(w1s_done, 1)
                for k in range(WGROUP):
                    c = g * WGROUP + k
                    src = w0s[:, 4 * c:4 * c + 4, :] if c < C0 else w1s[:, 2 * (c - C0):2 * (c - C0) + 2, :]
                    last = nc.tensor.transpose(w_bank(g)[:, k, :], src, ident)
                last.then_inc(transposed, 1)
            pe.wait_ge(b_in, 16 * 3)
            for g in range(BG):
                last = nc.tensor.transpose(out0[0:ND, g * P:(g + 1) * P], dense_sb[:, g, :], ident)
            last.then_inc(dense_t_done, 1)
            pe.wait_ge(sel_done, 1)
            pe.wait_ge(w_lo_done, WGROUPS)

            def spread_group(i, model, s):
                layer, chunks, _, _ = SLOTS[s]
                if s == FIRST0:
                    pe.wait_ge(x_in[model % NBUF], landed(i, model, LOADS))
                for old in last_in_banks(i, model, s):
                    if old[2] in POOL_SLOTS:
                        pe.wait_ge(mult_done, number(*old) + 1)
                    else:
                        pe.wait_ge(dve_lo_done, number(*old, ("vector",)) + 1)
                for at, c in enumerate(chunks):
                    if layer == 0:
                        w, x = sel[:, c, :], parts[:, model % NBUF, :]
                    else:
                        q, buf = c // (C1 // Q), (model - 1) % NBUF
                        w, x = sel[32 * q:32 * q + 32, C0 + c % (C1 // Q), :], parts[32 * q:32 * q + 32, buf, :]
                    last = nc.tensor.matmul(spread_of(s)[:, at, :], w, x, start=True, stop=True)
                last.then_inc(spread_done, 1)

            def products(i, model, s):
                layer, chunks, kind, _ = SLOTS[s]
                buf, base, out_bank = part_buffer(model, s), (0, C0)[layer], (out0, out1)[layer]
                if s == FIRST0 and model > 0:
                    pe.wait_ge(hid_done, i)
                if s == FIRST1 and model > 1:
                    pe.wait_ge(out1_read, i - 1)
                pe.wait_ge(pool_lo_done if kind == "pool" else dve_lo_done, number(i, model, s, (kind,)) + 1)
                passes = []
                for at, c in enumerate(chunks):
                    passes.append((w_hi[:, base + c, :], z_hi[:, buf, at, :]))
                    if not (layer == 0 and c == C0 - 1):
                        passes.append((w_lo[:, base + c, :], z_hi[:, buf, at, :]))
                        passes.append((w_hi[:, base + c, :], z_lo[:, buf, at, :]))
                for m, (w, x) in enumerate(passes):
                    last = nc.tensor.matmul(out_bank[:, :], w, x, start=(s in (FIRST0, FIRST1) and m == 0),
                                            stop=(s in (LAST0, LAST1) and m == len(passes) - 1))
                last.then_inc(prod_done, 1)

            def body(i, model):
                for s in slots_of(model, TILES):
                    spread_group(i, model, s)
                    if (old := before(i, model, s, LAG)) and old[1] > 0:
                        products(*old)
                    if (model, s) == (1, FIRST1 - 1):
                        pe.wait_ge(rem_w_done, 1)
                        pe.wait_ge(dense_done, 1)
                        for s0 in slots_of(0, TILES):
                            products(0, 0, s0)

            iterations(pe, body)
            for _, s in everything[-LAG:]:
                products(TILES, TILES, s)

            pe.wait_ge(m_in, 16 * 7)
            pe.wait_ge(sum0_done, TILES)
            pe.wait_ge(sum1_done, TILES)
            for k in range(K1):
                nc.tensor.matmul(mlp1(k), wtA[:, k * P:(k + 1) * P], zA[:, :], start=True, stop=False)
                nc.tensor.matmul(mlp1(k), wtB[:, k * P:(k + 1) * P], zB[:, :], start=False, stop=True).then_inc(m1_done, 1)
            for j in range(K2):
                for k in range(K1):
                    pe.wait_ge(h1_done, k + 1)
                    last = nc.tensor.matmul(mlp2(j), wt2[:, k, j * P:(j + 1) * P], h1[:, k, :], start=(k == 0), stop=(k == K1 - 1))
                last.then_inc(m2_done, 1)
            for k in range(K2):
                pe.wait_ge(h2_done, k + 1)
                last = nc.tensor.matmul(mlp3, wt3[:, k:k + 1], h2[:, k, :], start=(k == 0), stop=(k == K2 - 1))
            last.then_inc(m3_done, 1)


_WEIGHTS = ["W_top1", "b_top1", "W_top2", "b_top2", "W_top3", "L0_rec_W0", "L0_rec_b0", "L0_rec_W1", "L0_rec_b1"]


def kernel(**inputs):
    import numpy as _np
    import concourse.bacc as _bacc
    from concourse import mybir as _mybir
    from concourse.bass_utils import run_bass_kernel_spmd as _run

    nc = _bacc.Bacc("TRN2", target_bir_lowering=False, num_devices=1)
    arrays = {}

    def give(name, a):
        arrays[f"in_{name}"] = a
        return nc.dram_tensor(f"in_{name}", a.shape, _mybir.dt.from_np(a.dtype), kind="ExternalInput").ap()

    tables = [inputs[f"tbl_{f}"] for f in range(F)]
    starts = _np.cumsum([0] + [t.shape[0] for t in tables])[:F].astype(_np.int32)
    assert sum(t.shape[0] for t in tables) < 2 ** 24
    dense = give("dense_ctx", _np.ascontiguousarray(inputs["dense_ctx"]))
    lists = _np.asarray(inputs["ids"]).reshape(-1, P // F, TB * F // P, F).transpose(1, 3, 0, 2)
    ids = give("ids", _np.ascontiguousarray(lists.reshape(P, -1)))
    offsets = give("offsets", _np.ascontiguousarray(_np.tile(starts, P // F)[:, None]))
    table = give("tables", _np.concatenate(tables, axis=0))
    weights = [give(name, _np.ascontiguousarray(inputs[name])) for name in _WEIGHTS]
    consts = give("constants", constants())
    out = nc.dram_tensor("out", (inputs["ids"].shape[0], 1), _mybir.dt.float32, kind="ExternalOutput").ap()
    dlrm_tower(nc, dense, ids, offsets, table, *weights, consts, out)
    r = _run(nc, [arrays], core_ids=[0])
    return r.results[0]["out"]
```
